# Optimizing a Trainium2 kernel written in Bass

```python
import numpy as np
import jax
import jax.numpy as jnp

def _softmax(x, axis=-1):
    return jax.nn.softmax(x, axis=axis)

def _gelu(x):
    return jax.nn.gelu(x, approximate=True)

def _silu(x):
    return jax.nn.silu(x)

def _sigmoid(x):
    return jax.nn.sigmoid(x)

def _layernorm(x, axis=-1, eps=1e-05):
    m = jnp.mean(x, axis=axis, keepdims=True)
    v = jnp.var(x, axis=axis, keepdims=True)
    return (x - m) / jnp.sqrt(v + eps)

def _scatter_add(tgt, idx, src, axis=0):
    return tgt.at[idx].add(src)

def _segment_sum(src, seg, n):
    return jax.ops.segment_sum(src, seg, n)
kernel_name = 'mk_adaln_attn_ffn_d1_seqx_r4_e62998'

def setup_inputs(seed: int=0):
    np.random.seed(seed)
    _w = jnp.asarray

    def _rec_inputs():
        import jax
        import jax.numpy as jnp
        _rk = jax.random.key(seed)
        x = -0.0002928 + 1 * jax.random.normal(jax.random.fold_in(_rk, 1), (32, 64, 256), jnp.float32)
        _lenS = 64 - jax.random.randint(jax.random.fold_in(_rk, 7), (32,), 0, max(1, 64 // 4) + 1, jnp.int32)
        _lenS2 = 64 - jax.random.randint(jax.random.fold_in(_rk, 8), (32,), 0, max(1, 64 // 4) + 1, jnp.int32)
        cond_64 = -0.0184271 + 1.00439 * jax.random.normal(jax.random.fold_in(_rk, 12), (32, 64), jnp.float32)
        _validS = jnp.arange(64)[None, :] < _lenS[:, None]
        _validS2 = jnp.arange(64)[None, :] < _lenS2[:, None]
        _causal = jnp.tril(jnp.ones((64, 64), dtype=bool))
        mask_BxS_bf1 = jnp.ones((32, 64), dtype=bool)
        return (x, cond_64, mask_BxS_bf1)
    x, cond_64, mask_BxS_bf1 = _rec_inputs()

    def _L0_cond_setup():
        import jax, jax.numpy as jnp
        import numpy as np
        DIM = 256
        HEADS = 16
        DIM_HEAD = 64
        SCALE = 8.0

        def ln(x, g, eps=1e-05):
            mean = x.mean(axis=-1, keepdims=True)
            var = ((x - mean) ** 2).mean(axis=-1, keepdims=True)
            return (x - mean) * jax.lax.rsqrt(var + eps) * g

        def l2norm(t):
            n = jnp.maximum(jnp.linalg.norm(t, axis=-1, keepdims=True), 1e-12)
            return t / n

        def rel_pos_bias(n, w0, b0, g0, w1, b1, g1, w2, b2, dtype):
            pos = jnp.arange(-n + 1, n, dtype=dtype)[:, None]
            h = jax.nn.silu(ln(pos @ w0 + b0, g0))
            h = jax.nn.silu(ln(h @ w1 + b1, g1))
            h = h @ w2 + b2
            i = jnp.arange(n)
            idx = i[:, None] - i[None, :] + n - 1
            bias = h[idx]
            return jnp.transpose(bias, (2, 0, 1))
        key = jax.random.key(seed)
        ks = jax.random.split(key, 16)
        b, n = (2, 512)
        inner = HEADS * DIM_HEAD
        s = 0.02
        return {'x': jax.random.normal(ks[0], (b, n, DIM), jnp.float32), 'mask': jnp.ones((b, n), dtype=bool), 'g_norm': jnp.ones((DIM,), jnp.float32), 'Wq': jax.random.normal(ks[1], (DIM, inner), jnp.float32) * s, 'Wkv': jax.random.normal(ks[2], (DIM, 2 * DIM_HEAD), jnp.float32) * s, 'q_scale': jnp.ones((DIM_HEAD,), jnp.float32), 'k_scale': jnp.ones((DIM_HEAD,), jnp.float32), 'null_kv': jax.random.normal(ks[3], (2, DIM_HEAD), jnp.float32), 'null_attn_bias': jax.random.normal(ks[4], (HEADS,), jnp.float32), 'w0': jax.random.normal(ks[5], (1, DIM), jnp.float32) * s, 'b0': jnp.zeros((DIM,), jnp.float32), 'g0': jnp.ones((DIM,), jnp.float32), 'w1': jax.random.normal(ks[6], (DIM, DIM), jnp.float32) * s, 'b1': jnp.zeros((DIM,), jnp.float32), 'g1': jnp.ones((DIM,), jnp.float32), 'w2': jax.random.normal(ks[7], (DIM, HEADS), jnp.float32) * s, 'b2': jnp.zeros((HEADS,), jnp.float32), 'Wout': jax.random.normal(ks[8], (inner, DIM), jnp.float32) * s, 'g_out': jnp.ones((DIM,), jnp.float32)}
    _L0_cond_all = _L0_cond_setup()
    _L0_cond_in = {k: v for k, v in _L0_cond_all.items() if k in ('g_norm', 'Wq', 'Wkv', 'q_scale', 'k_scale', 'null_attn_bias', 'w0', 'b0', 'g0', 'w1', 'b1', 'g1', 'w2', 'b2', 'Wout', 'g_out')}
    del _L0_cond_all

    def _L0_attn_setup():
        import math
        import jax, jax.numpy as jnp
        import numpy as np
        DIM = 256
        key = jax.random.key(seed)
        ks = jax.random.split(key, 5)
        B, T, d = (4, 1024, DIM)
        x = jax.random.normal(ks[0], (B, T, d), dtype=jnp.float32)
        std = 0.02
        Wq = jax.random.normal(ks[1], (d, d), dtype=jnp.float32) * std
        Wk = jax.random.normal(ks[2], (d, d), dtype=jnp.float32) * std
        Wv = jax.random.normal(ks[3], (d, d), dtype=jnp.float32) * std
        Wo = jax.random.normal(ks[4], (d, d), dtype=jnp.float32) * std
        decay_logit = jnp.asarray(3.0, dtype=jnp.float32)
        out_scale = jnp.asarray(0.1, dtype=jnp.float32)
        return {'x': x, 'Wq': Wq, 'Wk': Wk, 'Wv': Wv, 'Wo': Wo, 'decay_logit': decay_logit, 'out_scale': out_scale}
    _L0_attn_all = _L0_attn_setup()
    _L0_attn_in = {k: v for k, v in _L0_attn_all.items() if k in ('Wq', 'Wk', 'Wv', 'Wo', 'decay_logit', 'out_scale')}
    del _L0_attn_all

    def _L0_cond2_setup():
        import jax, jax.numpy as jnp
        import numpy as np
        B, S, H = (4, 512, 256)
        E = 8
        M = 128
        K = 2
        N_SHARED = 2
        SM = M * N_SHARED
        G = 64
        GE_TEMP = 1.0
        ALPHA = 0.001
        SEQ_AUX = True
        NORM_TOPK = True
        COS_TEMP = 0.78
        CONS_ALPHA = 0.01
        LEAKY_SLOPE = 0.01
        EPS_COS = 1e-08

        def _leaky(x):
            return jnp.where(x >= 0, x, LEAKY_SLOPE * x)

        def _moe_forward(hidden_states, g, wt, wg, w_gate, w_up, w_down, sw_gate, sw_up, sw_down):
            b, s, h = hidden_states.shape
            x = hidden_states.reshape(-1, h)
            T = x.shape[0]
            logits_h = x @ wt.T
            logits_g = g @ wg.T
            logits_g = jnp.repeat(logits_g, s, axis=0)
            logits = (logits_h + logits_g / GE_TEMP) / (1.0 + 1.0 / GE_TEMP)
            scores = jax.nn.softmax(logits, axis=-1)
            topk_w, topk_idx = jax.lax.top_k(scores, K)
            if K > 1 and NORM_TOPK:
                topk_w = topk_w / (topk_w.sum(-1, keepdims=True) + 1e-20)
            onehot = jax.nn.one_hot(topk_idx.reshape(b, s * K), E, dtype=jnp.float32)
            ce = onehot.sum(1) / (s * K / E)
            aux_loss = (ce * scores.reshape(b, s, E).mean(1)).sum(1).mean() * ALPHA
            gp = _leaky(jnp.einsum('th,ehm->etm', x, w_gate))
            up = jnp.einsum('th,ehm->etm', x, w_up)
            y_all = jnp.einsum('etm,emh->eth', gp * up, w_down)
            y_sel = y_all[topk_idx, jnp.arange(T)[:, None], :]
            y = (y_sel * topk_w[..., None]).sum(1).reshape(b, s, h)
            p = _leaky(hidden_states @ sw_gate) * (hidden_states @ sw_up) @ sw_down
            y = y + p
            num = jnp.sum(y * p, -1)
            den = jnp.maximum(jnp.linalg.norm(y, axis=-1), EPS_COS) * jnp.maximum(jnp.linalg.norm(p, axis=-1), EPS_COS)
            closs = CONS_ALPHA * jnp.mean(num / den / (1.0 + COS_TEMP))
            return (y, aux_loss + closs)
        key = jax.random.key(seed)
        ks = jax.random.split(key, 12)
        sh = 1.0 / np.sqrt(H)
        sm = 1.0 / np.sqrt(M)
        ssm = 1.0 / np.sqrt(SM)
        sg = 1.0 / np.sqrt(G)
        return {'hidden_states': jax.random.normal(ks[0], (B, S, H), jnp.float32), 'g': jax.random.normal(ks[1], (B, G), jnp.float32), 'wt': jax.random.uniform(ks[2], (E, H), jnp.float32, -sh, sh), 'wg': jax.random.uniform(ks[3], (E, G), jnp.float32, -sg, sg), 'w_gate': jax.random.uniform(ks[4], (E, H, M), jnp.float32, -sh, sh), 'w_up': jax.random.uniform(ks[5], (E, H, M), jnp.float32, -sh, sh), 'w_down': jax.random.uniform(ks[6], (E, M, H), jnp.float32, -sm, sm), 'sw_gate': jax.random.uniform(ks[7], (H, SM), jnp.float32, -sh, sh), 'sw_up': jax.random.uniform(ks[8], (H, SM), jnp.float32, -sh, sh), 'sw_down': jax.random.uniform(ks[9], (SM, H), jnp.float32, -ssm, ssm)}
    _L0_cond2_all = _L0_cond2_setup()
    _L0_cond2_in = {k: v for k, v in _L0_cond2_all.items() if k in ('wt', 'wg', 'w_gate', 'w_up', 'w_down', 'sw_gate', 'sw_up', 'sw_down')}
    del _L0_cond2_all

    def _L0_ffn_setup():
        import jax, jax.numpy as jnp
        import numpy as np
        HIDDEN = 256
        INTER = 1024
        key = jax.random.key(seed)
        k1, k2, k3, k4, k5 = jax.random.split(key, 5)
        hidden_states = jax.random.normal(k1, (4, 512, HIDDEN), dtype=jnp.float32)
        W1 = jax.random.normal(k2, (HIDDEN, INTER), dtype=jnp.float32) * (1.0 / np.sqrt(HIDDEN))
        b1 = jax.random.normal(k3, (INTER,), dtype=jnp.float32) * 0.02
        W2 = jax.random.normal(k4, (INTER, HIDDEN), dtype=jnp.float32) * (1.0 / np.sqrt(INTER))
        b2 = jax.random.normal(k5, (HIDDEN,), dtype=jnp.float32) * 0.02
        return {'hidden_states': hidden_states, 'W1': W1, 'b1': b1, 'W2': W2, 'b2': b2}
    _L0_ffn_all = _L0_ffn_setup()
    _L0_ffn_in = {k: v for k, v in _L0_ffn_all.items() if k in ('W1', 'b1', 'W2', 'b2')}
    del _L0_ffn_all
    return {'x': x, 'cond_64': cond_64, 'mask_BxS_bf1': mask_BxS_bf1, 'L0_cond_g_norm': _L0_cond_in['g_norm'], 'L0_cond_Wq': _L0_cond_in['Wq'], 'L0_cond_Wkv': _L0_cond_in['Wkv'], 'L0_cond_q_scale': _L0_cond_in['q_scale'], 'L0_cond_k_scale': _L0_cond_in['k_scale'], 'L0_cond_null_attn_bias': _L0_cond_in['null_attn_bias'], 'L0_cond_w0': _L0_cond_in['w0'], 'L0_cond_b0': _L0_cond_in['b0'], 'L0_cond_g0': _L0_cond_in['g0'], 'L0_cond_w1': _L0_cond_in['w1'], 'L0_cond_b1': _L0_cond_in['b1'], 'L0_cond_g1': _L0_cond_in['g1'], 'L0_cond_w2': _L0_cond_in['w2'], 'L0_cond_b2': _L0_cond_in['b2'], 'L0_cond_Wout': _L0_cond_in['Wout'], 'L0_cond_g_out': _L0_cond_in['g_out'], 'L0_attn_Wq': _L0_attn_in['Wq'], 'L0_attn_Wk': _L0_attn_in['Wk'], 'L0_attn_Wv': _L0_attn_in['Wv'], 'L0_attn_Wo': _L0_attn_in['Wo'], 'L0_attn_decay_logit': _L0_attn_in['decay_logit'], 'L0_attn_out_scale': _L0_attn_in['out_scale'], 'L0_cond2_wt': _L0_cond2_in['wt'], 'L0_cond2_wg': _L0_cond2_in['wg'], 'L0_cond2_w_gate': _L0_cond2_in['w_gate'], 'L0_cond2_w_up': _L0_cond2_in['w_up'], 'L0_cond2_w_down': _L0_cond2_in['w_down'], 'L0_cond2_sw_gate': _L0_cond2_in['sw_gate'], 'L0_cond2_sw_up': _L0_cond2_in['sw_up'], 'L0_cond2_sw_down': _L0_cond2_in['sw_down'], 'L0_ffn_W1': _L0_ffn_in['W1'], 'L0_ffn_b1': _L0_ffn_in['b1'], 'L0_ffn_W2': _L0_ffn_in['W2'], 'L0_ffn_b2': _L0_ffn_in['b2']}

def reference(x, cond_64, mask_BxS_bf1, L0_cond_g_norm, L0_cond_Wq, L0_cond_Wkv, L0_cond_q_scale, L0_cond_k_scale, L0_cond_null_attn_bias, L0_cond_w0, L0_cond_b0, L0_cond_g0, L0_cond_w1, L0_cond_b1, L0_cond_g1, L0_cond_w2, L0_cond_b2, L0_cond_Wout, L0_cond_g_out, L0_attn_Wq, L0_attn_Wk, L0_attn_Wv, L0_attn_Wo, L0_attn_decay_logit, L0_attn_out_scale, L0_cond2_wt, L0_cond2_wg, L0_cond2_w_gate, L0_cond2_w_up, L0_cond2_w_down, L0_cond2_sw_gate, L0_cond2_sw_up, L0_cond2_sw_down, L0_ffn_W1, L0_ffn_b1, L0_ffn_W2, L0_ffn_b2):
    import jax
    import jax.numpy as jnp

    def _L0_cond_ref(x, mask, g_norm, Wq, Wkv, q_scale, k_scale, null_kv, null_attn_bias, w0, b0, g0, w1, b1, g1, w2, b2, Wout, g_out):
        import jax, jax.numpy as jnp
        import numpy as np
        DIM = 256
        HEADS = 16
        DIM_HEAD = 64
        SCALE = 8.0

        def ln(x, g, eps=1e-05):
            mean = x.mean(axis=-1, keepdims=True)
            var = ((x - mean) ** 2).mean(axis=-1, keepdims=True)
            return (x - mean) * jax.lax.rsqrt(var + eps) * g

        def l2norm(t):
            n = jnp.maximum(jnp.linalg.norm(t, axis=-1, keepdims=True), 1e-12)
            return t / n

        def rel_pos_bias(n, w0, b0, g0, w1, b1, g1, w2, b2, dtype):
            pos = jnp.arange(-n + 1, n, dtype=dtype)[:, None]
            h = jax.nn.silu(ln(pos @ w0 + b0, g0))
            h = jax.nn.silu(ln(h @ w1 + b1, g1))
            h = h @ w2 + b2
            i = jnp.arange(n)
            idx = i[:, None] - i[None, :] + n - 1
            bias = h[idx]
            return jnp.transpose(bias, (2, 0, 1))
        b, n, _ = x.shape
        xn = ln(x, g_norm)
        q = (xn @ Wq).reshape(b, n, HEADS, DIM_HEAD).transpose(0, 2, 1, 3)
        kv = xn @ Wkv
        k, v = (kv[..., :DIM_HEAD], kv[..., DIM_HEAD:])
        nk = jnp.broadcast_to(null_kv[0], (b, 1, DIM_HEAD))
        nv = jnp.broadcast_to(null_kv[1], (b, 1, DIM_HEAD))
        k = jnp.concatenate([nk, k], axis=1)
        v = jnp.concatenate([nv, v], axis=1)
        q = l2norm(q) * q_scale
        k = l2norm(k) * k_scale
        sim = jnp.einsum('bhid,bjd->bhij', q, k) * SCALE
        bias = rel_pos_bias(n, w0, b0, g0, w1, b1, g1, w2, b2, q.dtype)
        null_bias = jnp.broadcast_to(null_attn_bias[:, None, None], (HEADS, n, 1))
        attn_bias = jnp.concatenate([null_bias, bias], axis=-1)
        sim = sim + attn_bias
        neg = -jnp.finfo(sim.dtype).max
        causal = jnp.triu(jnp.ones((n, n + 1), dtype=bool), k=2)
        sim = jnp.where(causal, neg, sim)
        m = jnp.pad(mask, ((0, 0), (1, 0)), constant_values=True)[:, None, None, :]
        sim = jnp.where(m, sim, neg)
        attn = jax.nn.softmax(sim, axis=-1)
        out = jnp.einsum('bhij,bjd->bhid', attn, v)
        out = out.transpose(0, 2, 1, 3).reshape(b, n, HEADS * DIM_HEAD)
        return ln(out @ Wout, g_out)

    def _L0_attn_ref(x, Wq, Wk, Wv, Wo, decay_logit, out_scale):
        import math
        import jax, jax.numpy as jnp
        import numpy as np
        DIM = 256
        B, T, d = x.shape
        scale = 1.0 / math.sqrt(d)
        q = x @ Wq.T
        k = x @ Wk.T
        v = x @ Wv.T
        scores = jnp.einsum('btd,bsd->bts', q, k) * scale
        decay = jax.nn.sigmoid(decay_logit)
        pos = jnp.arange(T)
        diff = pos[None, :] - pos[:, None]
        mask = (diff > 0).astype(x.dtype)
        expo = jnp.maximum(diff.astype(x.dtype) - 1.0, 0.0)
        weights = decay ** expo * mask
        scores = scores * weights[None, :, :]
        retrieved = jnp.einsum('bts,bsd->btd', scores, v)
        return retrieved @ Wo.T * out_scale

    def _L0_cond2_ref(hidden_states, g, wt, wg, w_gate, w_up, w_down, sw_gate, sw_up, sw_down):
        import jax, jax.numpy as jnp
        import numpy as np
        B, S, H = (4, 512, 256)
        E = 8
        M = 128
        K = 2
        N_SHARED = 2
        SM = M * N_SHARED
        G = 64
        GE_TEMP = 1.0
        ALPHA = 0.001
        SEQ_AUX = True
        NORM_TOPK = True
        COS_TEMP = 0.78
        CONS_ALPHA = 0.01
        LEAKY_SLOPE = 0.01
        EPS_COS = 1e-08

        def _leaky(x):
            return jnp.where(x >= 0, x, LEAKY_SLOPE * x)

        def _moe_forward(hidden_states, g, wt, wg, w_gate, w_up, w_down, sw_gate, sw_up, sw_down):
            b, s, h = hidden_states.shape
            x = hidden_states.reshape(-1, h)
            T = x.shape[0]
            logits_h = x @ wt.T
            logits_g = g @ wg.T
            logits_g = jnp.repeat(logits_g, s, axis=0)
            logits = (logits_h + logits_g / GE_TEMP) / (1.0 + 1.0 / GE_TEMP)
            scores = jax.nn.softmax(logits, axis=-1)
            topk_w, topk_idx = jax.lax.top_k(scores, K)
            if K > 1 and NORM_TOPK:
                topk_w = topk_w / (topk_w.sum(-1, keepdims=True) + 1e-20)
            onehot = jax.nn.one_hot(topk_idx.reshape(b, s * K), E, dtype=jnp.float32)
            ce = onehot.sum(1) / (s * K / E)
            aux_loss = (ce * scores.reshape(b, s, E).mean(1)).sum(1).mean() * ALPHA
            gp = _leaky(jnp.einsum('th,ehm->etm', x, w_gate))
            up = jnp.einsum('th,ehm->etm', x, w_up)
            y_all = jnp.einsum('etm,emh->eth', gp * up, w_down)
            y_sel = y_all[topk_idx, jnp.arange(T)[:, None], :]
            y = (y_sel * topk_w[..., None]).sum(1).reshape(b, s, h)
            p = _leaky(hidden_states @ sw_gate) * (hidden_states @ sw_up) @ sw_down
            y = y + p
            num = jnp.sum(y * p, -1)
            den = jnp.maximum(jnp.linalg.norm(y, axis=-1), EPS_COS) * jnp.maximum(jnp.linalg.norm(p, axis=-1), EPS_COS)
            closs = CONS_ALPHA * jnp.mean(num / den / (1.0 + COS_TEMP))
            return (y, aux_loss + closs)
        y, _ = _moe_forward(hidden_states, g, wt, wg, w_gate, w_up, w_down, sw_gate, sw_up, sw_down)
        return y

    def _L0_ffn_ref(hidden_states, W1, b1, W2, b2):
        import jax, jax.numpy as jnp
        import numpy as np
        HIDDEN = 256
        INTER = 1024
        h = jax.nn.relu(jnp.einsum('bsh,hi->bsi', hidden_states, W1) + b1)
        return jnp.einsum('bsi,ih->bsh', h, W2) + b2
    x = x + _L0_attn_ref(_L0_cond_ref(x, mask_BxS_bf1, L0_cond_g_norm, L0_cond_Wq, L0_cond_Wkv, L0_cond_q_scale, L0_cond_k_scale, cond_64, L0_cond_null_attn_bias, L0_cond_w0, L0_cond_b0, L0_cond_g0, L0_cond_w1, L0_cond_b1, L0_cond_g1, L0_cond_w2, L0_cond_b2, L0_cond_Wout, L0_cond_g_out), L0_attn_Wq, L0_attn_Wk, L0_attn_Wv, L0_attn_Wo, L0_attn_decay_logit, L0_attn_out_scale)
    x = x + _L0_ffn_ref(_L0_cond2_ref(x, cond_64, L0_cond2_wt, L0_cond2_wg, L0_cond2_w_gate, L0_cond2_w_up, L0_cond2_w_down, L0_cond2_sw_gate, L0_cond2_sw_up, L0_cond2_sw_down), L0_ffn_W1, L0_ffn_b1, L0_ffn_W2, L0_ffn_b2)
    return x

_drawn_inputs = setup_inputs


def setup_inputs(seed=0):
    import zlib

    import numpy as np

    out = dict(_drawn_inputs(seed))
    spreads = {'L0_cond_g_norm': (1.0, 0.6),
     'L0_cond_q_scale': (1.0, 0.6),
     'L0_cond_k_scale': (1.0, 0.6),
     'L0_cond_b0': (0.0, 0.8),
     'L0_cond_g0': (1.0, 0.6),
     'L0_cond_b1': (0.0, 0.8),
     'L0_cond_g1': (1.0, 0.6),
     'L0_cond_b2': (0.0, 0.8),
     'L0_cond_g_out': (1.0, 0.6)}
    factors = {'L0_cond_Wq': 8.0,
     'L0_cond_Wkv': 6.828,
     'L0_cond_null_attn_bias': 8.0,
     'L0_cond_w0': 8.0,
     'L0_cond_w1': 8.0,
     'L0_cond_w2': 8.0,
     'L0_cond_Wout': 6.093,
     'L0_attn_Wq': 6.839,
     'L0_attn_Wk': 6.72,
     'L0_attn_Wv': 6.523,
     'L0_attn_Wo': 6.534,
     'L0_ffn_b1': 4.122,
     'L0_ffn_b2': 2.929}
    for name, (base, spread) in spreads.items():
        noise = np.random.default_rng([zlib.crc32(name.encode()), seed]).standard_normal(out[name].shape)
        drawn = base * np.exp(spread * noise) if base else spread * noise
        out[name] = jnp.asarray(drawn.astype(out[name].dtype))
    for name, factor in factors.items():
        out[name] = (out[name] * factor).astype(out[name].dtype)
    return out
```

```python
import concourse.bass as bass
from concourse import mybir
from contextlib import ExitStack

F32 = mybir.dt.float32
F32R = mybir.dt.float32r
U32 = mybir.dt.uint32
U8 = mybir.dt.uint8
ALU = mybir.AluOpType
ACT = mybir.ActivationFunctionType
AX_X = mybir.AxisListType.X

P = 128
B, S, D = 32, 64, 256
T = B * S
NT = T // P
KD = D // P
H, DH = 16, 64
HP = H // 2
NK = S + 1
QKV = H * DH + 2 * DH
NB3 = 3
QB = QKV // NB3
QH = QB // DH
PB = QH // 2
E, M = 8, 128
NS = 2
U = NS + E
INTER = 1024
FB = INTER // P
G = 4
GT = T // G
TG = GT // P
SB = GT // S
BIG = 1.5e38
EPS = 1e-5
BANK = 512



def adaln_attention_ffn(nc, a, out):
    ctx = ExitStack()
    with ctx:
        def sb(name, shape, dt=F32, scope=ctx):
            return scope.enter_context(nc.sbuf_tensor(name, shape, dt))

        xs = sb("xs", [P, NT, D])
        ident = sb("ident", [P, P])
        wu_h = sb("wu_h", [P, U, 3 * D], F32R)
        wt_h = sb("wt_h", [P, KD, P], F32R)
        wt_l = sb("wt_l", [P, KD, P], F32R)
        wgT = sb("wgT", [DH, P])
        condT = sb("condT", [DH, B])
        sel = sb("sel", [2 * E, E, P], F32R)
        iota_e = sb("iota_e", [P, E])
        b1c = sb("b1c", [P, FB])
        b2r = sb("b2r", [P, D])
        carrier = sb("carrier", [P, 1])

        with ExitStack() as early:
            raw_qkv = sb("raw_qkv", [P, KD, QKV], scope=early)
            raw_out = sb("raw_out", [P, HP, D], scope=early)
            raw_att = sb("raw_att", [P, 4, KD, D], scope=early)
            raw_w1 = sb("raw_w1", [P, KD, D], scope=early)
            woT = sb("woT", [P, KD, D], scope=early)
        wu_l = sb("wu_l", [P, U, 3 * D], F32R)

        with ExitStack() as first:
            def s1(name, shape, dt=F32):
                return sb(name, shape, dt, first)
            stage = s1("stage", [P, 3 * D])
            wqkv_h = s1("wqkv_h", [P, KD, QKV], F32R)
            wqkv_l = s1("wqkv_l", [P, KD, QKV], F32R)
            wout_h = s1("wout_h", [P, HP, D], F32R)
            wout_l = s1("wout_l", [P, HP, D], F32R)
            mqk = s1("mqk", [P, KD, D])
            wvo_h = s1("wvo_h", [P, KD, D], F32R)
            wvo_l = s1("wvo_l", [P, KD, D], F32R)
            nvw = s1("nvw", [H, D])
            nvsel = s1("nvsel", [P, HP, H])
            bias = s1("bias", [P, H, NK])
            biasm = s1("biasm", [P, H, NK])
            mneg = s1("mneg", [P, NT, NK])
            decay = s1("decay", [P, P])
            colsc = s1("colsc", [P, 32])
            ones = s1("ones", [P, 1])
            half = s1("half", [P, H + 1])
            st6 = s1("st6", [P, 2, 6])
            mv = s1("mv", [P, 2, 2])
            ve1 = s1("ve1", [P, 1])
            ve2 = s1("ve2", [P, 1])
            rs1 = s1("rs1", [P, 1])
            rs2 = s1("rs2", [P, 1])
            xn = s1("xn", [P, D])
            xnT_h = s1("xnT_h", [P, KD, P], F32R)
            xnT_l = s1("xnT_l", [P, KD, P], F32R)
            sq = s1("sq", [P, H + 1, DH])
            ss = s1("ss", [P, H + 1])
            sc = s1("sc", [P, H + 1])
            rn = s1("rn", [P, H + 1])
            qn = s1("qn", [P, H, DH])
            kn2 = s1("kn2", [P, 2, DH])
            qT = s1("qT", [P, HP, P])
            kT = s1("kT", [P, P])
            kblk = s1("kblk", [P, 2, 2 * NK])
            vblk_h = s1("vblk_h", [P, 2, 2, P], F32R)
            vblk_l = s1("vblk_l", [P, 2, 2, P], F32R)
            sim = s1("sim", [P, H, NK])
            mx = s1("mx", [P, H])
            pe = s1("pe", [P, H, NK])
            den = s1("den", [P, H])
            rden = s1("rden", [P, H])
            pr = s1("pr", [P, H * NK])
            pnT = s1("pnT", [H, P])
            zn = s1("zn", [P, 2, D])
            znT = s1("znT", [P, KD, P])
            uT = s1("uT", [P, KD, P])
            at = s1("at", [P, P])
            rT_h = s1("rT_h", [P, KD, P], F32R)
            rT_l = s1("rT_l", [P, KD, P], F32R)
            with ExitStack() as early2:
                def s2(name, shape, dt=F32):
                    return sb(name, shape, dt, early2)
                rows = s2("rows", [DH, 5, D])
                h0 = s2("h0", [DH, D])
                h1 = s2("h1", [DH, D])
                hT = s2("hT", [P, KD, DH])
                w2p = s2("w2p", [P, KD, H])
                b2h = s2("b2h", [DH, H])
                relp = s2("relp", [DH, H])
                relT = s2("relT", [H, 2 * DH])
                goutr = s2("goutr", [P, D])
                wvo_f = s2("wvo_f", [P, KD, D])
                wt_raw = s2("wt_raw", [P, KD, P])
                nkB = s2("nkB", [P, DH])
                nksq = s2("nksq", [P, DH])
                nullb = s2("nullb", [P, H])
                mask_u = s2("mask_u", [P, NT, S], U8)
                zeros = s2("zeros", [P, 2 * P])
            pT_h = s1("pT_h", [P, HP, P], F32R)
            pT_l = s1("pT_l", [P, HP, P], F32R)
            oT_h = s1("oT_h", [P, HP, P], F32R)
            oT_l = s1("oT_l", [P, HP, P], F32R)

        w1_h = sb("w1_h", [P, KD, INTER], F32R)
        w1_l = sb("w1_l", [P, KD, INTER], F32R)
        w2_h = sb("w2_h", [P, FB, D], F32R)
        w2_l = sb("w2_l", [P, FB, D], F32R)
        fstage = sb("fstage", [P, 4, 2 * BANK])
        xg = sb("xg", [P, TG, D])
        xb = sb("xb", [P, TG, D])
        x1T_h = sb("x1T_h", [P, KD, GT], F32R)
        x1T_l = sb("x1T_l", [P, KD, GT], F32R)
        lgT = sb("lgT", [E, GT])
        lg = sb("lg", [P, TG, E])
        lmax = sb("lmax", [P, TG])
        le = sb("le", [P, TG, E])
        lsum = sb("lsum", [P, TG])
        lrec = sb("lrec", [P, TG])
        score = sb("score", [P, TG, E])
        top = sb("top", [P, TG, 8])
        topi = sb("topi", [P, TG, 8], U32)
        topf = sb("topf", [P, TG, 8])
        tsum = sb("tsum", [P, TG])
        trec = sb("trec", [P, TG])
        topw = sb("topw", [P, TG, 2])
        wk = sb("wk", [P, 2, TG, E])
        wf = sb("wf", [P, TG, E])
        wr = sb("wr", [P, TG, E], F32R)
        wst = sb("wst", [P, TG, 2 * E])
        wT = sb("wT", [2 * E, GT], F32R)
        gs = sb("gs", [P, GT])
        lk = sb("lk", [P, GT])
        hu = sb("hu", [P, GT])
        hw = sb("hw", [P, 2, GT])
        hh = sb("hh", [P, 2, GT], F32R)
        hl = sb("hl", [P, 2, GT], F32R)
        yT_h = sb("yT_h", [P, KD, GT], F32R)
        yT_l = sb("yT_l", [P, KD, GT], F32R)
        obuf = sb("obuf", [P, TG, D])

        bank = [ctx.enter_context(nc.psum_tensor(f"bank{i}", [P, BANK], F32)) for i in range(8)]
        rel_dram = nc.dram_tensor("rel_scratch", (H, S, S), F32, kind="Internal")

        sems = {}
        for n in """ld_x0 ld_x1 ld_qkv ld_out ld_att ld_mlp ld_cols ld_mask ld_null ld_late st_rel ld_bias ld_u ld_f st_out
                    pc vc ac p_const p_nrn p_ln p_dec p_nkk p_bias p_mneg p_sel v_nss v_nkk v_ln v_hn v_hT v_rel
                    v_exp v_rawqkv v_wout v_mqk v_wvof v_wvo v_neglog v_ln_in v_lnd v_lin
                    a_sil a_qkvh a_wouth a_wvoh a_e1 a_e2 a_decay a_nvw a_wth v_wtl
                    t_hT t_mlp t_woT t_mqk t_vo t_nvw t_rel v_woT unit_h unit
                    st1 mv1 ln1_ve ln1_rs xn xnT xnT_h xnT_l qkv sq ss ss_c rn qn kn2 v_h
                    kT_t kT kblk vblk qT_t qT sim_t biasm sim mx simc pe den rden pr
                    pT_t pT_h pT_l pnT_t pnT av_t oT_h oT_l wo_t st2 mv2 ln2_ve ln2_rs zn
                    znT_t znT uT_t uT sc_t at rt_t rT_h rT_l vo_t x1
                    f_h f_l xg xb x1T_t x1T_h x1T_l lg_t lgT lgtr rv ra wst wT_t wT
                    gate_t up_t wb_t gs lk hu hw hh hl down_t yT_h yT_l f1_t fr fh fl f2_t obuf""".split():
            sems[n] = ctx.enter_context(nc.semaphore("s_" + n))

        def wait(e, name, count):
            if not isinstance(count, int) or count > 0:
                e.wait_ge(sems[name], count)

        def settle(e):
            e.memset(carrier[:, :], 0.0)

        def dma_wait(e, name, n):
            e.wait_ge(sems[name], 16 * n)

        def done(ins, name):
            ins.then_inc(sems[name], 1)

        def load(e, dst, src, name):
            e.dma_start(dst, src).then_inc(sems[name], 16)

        def chain(e, own):
            counts = {}

            def link(ins, name=own):
                counts[name] = counts.get(name, 0) + 1
                done(ins, name)
                e.wait_ge(sems[name], counts[name])
            return link

        GN, GO, KSC, QSC, DLG, OSC, NKC, NSS, NRN, KQS, LNV, LNR, POS, GOS, NKK, NX, MXN, ABX, EXA, LNA, LND, EX1 = (
            0, 2, 4, 5, 6, 7, 8, 9, 10, 11, 12, 13, 14, 15, 17, 18, 19, 20, 21, 22, 23, 24)

        def col(c, n=P):
            return colsc[0:n, c:c + 1]

        FIRST_I, LAST_I = -2, NT + 2
        STEADY0, STEADY1 = 4, NT - 3
        PAIRS = (STEADY1 - STEADY0 + 1) // 2

        def pipeline(e, body, extra=None):
            def edge(i):
                body(i, i % 2, lambda off: 0 <= i + off < NT)
            for i in range(FIRST_I, STEADY0):
                edge(i)
            with e.Fori(0, PAIRS) as r:
                for half_step in range(2):
                    body(2 * r + (STEADY0 + half_step), (STEADY0 + half_step) % 2, lambda off: True)
                if extra is not None:
                    extra(r)
            for i in range(STEADY0 + 2 * PAIRS, LAST_I + 1):
                edge(i)

        def groups(e, body):
            body(0)
            with e.Fori(1, G) as g:
                body(g)

        def span(lo, n):
            return slice(lo, lo + n) if isinstance(lo, int) else bass.ds(lo, n)

        def at_tile(t3, i):
            if isinstance(i, int):
                return t3[:, i, :]
            return t3[:, bass.ds(i, 1), :].rearrange("p o d -> p (o d)")

        def split_passes(e, dst, stat, mov, start, stop, **kw):
            e.matmul(dst, stat[0], mov[0], start=start, stop=False, **kw)
            e.matmul(dst, stat[0], mov[1], start=False, stop=False, **kw)
            return e.matmul(dst, stat[1], mov[0], start=False, stop=stop, **kw)

        RV_EXP = 3
        RV_PER_GROUP = RV_EXP + 14

        def round_unit(e, g, u):
            n, par = U * g + u, u % 2
            wait(e, "hw", n + 1)
            if u >= 2:
                wait(e, "down_t", n - 1)
            wait(e, "f2_t", FB * g)
            done(e.activation(hh[:, par, :], hw[:, par, :], ACT.Copy), "hh")

        block = ctx.enter_context(nc.Block())

        @block.sync
        def _(e):
            x_v = a["x"].rearrange("(t two) s d -> (two s) t d", two=2)

            def kp(name):
                return a[name].rearrange("(k p) n -> p k n", p=P)

            def row(name, n):
                return a[name].rearrange("(o d) -> o d", o=1).to_broadcast([n, a[name].shape[0]])

            load(e, xs[:, 0:4, :], x_v[:, 0:4, :], "ld_x0")
            load(e, raw_qkv[:, :, 0:H * DH], kp("c_Wq"), "ld_qkv")
            load(e, raw_qkv[:, :, H * DH:QKV], kp("c_Wkv"), "ld_qkv")
            load(e, rows[:, 0, :], a["c_w0"].to_broadcast([DH, D]), "ld_mlp")
            for n, name in enumerate(("c_b0", "c_g0", "c_b1", "c_g1")):
                load(e, rows[:, 1 + n, :], row(name, DH), "ld_mlp")
            load(e, raw_w1[:, :, :], kp("c_w1"), "ld_mlp")
            load(e, w2p[:, :, :], kp("c_w2"), "ld_mlp")
            load(e, b2h[:, :], row("c_b2", DH), "ld_mlp")
            mask_v = a["mask"].rearrange("(t two) s -> two t s", two=2)
            for b in range(2):
                load(e, mask_u[b * S:(b + 1) * S, :, :], mask_v[b:b + 1, :, :].to_broadcast([S, NT, S]), "ld_mask")
            load(e, raw_out[:, :, :], kp("c_Wout"), "ld_out")
            for n, name in enumerate(("t_Wq", "t_Wk", "t_Wv", "t_Wo")):
                load(e, raw_att[:, n, :, :], kp(name), "ld_att")
            load(e, goutr[:, :], row("c_g_out", P), "ld_att")
            load(e, xs[:, 4:NT, :], x_v[:, 4:NT, :], "ld_x1")
            wait(e, "p_const", 1)
            with nc.allow_non_contiguous_dma(reason="small transposed tables"):
                for k in range(KD):
                    load(e, wt_raw[:, k, 0:E], a["m_wt"][:, k * P:(k + 1) * P].rearrange("e p -> p e"), "ld_late")
                load(e, wgT[:, 0:E], a["m_wg"].rearrange("e g -> g e"), "ld_late")
                load(e, condT[:, :], a["cond"].rearrange("b g -> g b"), "ld_late")
                load(e, b1c[:, :], a["f_b1"].rearrange("(j p) -> p j", p=P), "ld_late")
            load(e, b2r[:, :], row("f_b2", P), "ld_late")
            wait(e, "v_rel", 1)
            ladder = relT[:, S - 1:2 * S - 1]
            ladder = bass.AP(tensor=ladder.tensor, offset=ladder.offset, ap=[ladder.ap[0], [-1, S], [1, S]])
            load(e, rel_dram.ap(), ladder, "st_rel")
            dma_wait(e, "st_rel", 1)
            for b in range(2):
                load(e, bias[b * S:(b + 1) * S, :, 0:S],
                     rel_dram.ap().rearrange("h i j -> i h j"), "ld_bias")

            gate_s = a["m_sg"].rearrange("(k p) (u m) -> p k u m", p=P, m=M)
            up_s = a["m_su"].rearrange("(k p) (u m) -> p k u m", p=P, m=M)
            down_s = a["m_sd"].rearrange("(u m) n -> m u n", m=M)
            gate_e = a["m_wgate"].rearrange("e (k p) m -> p k e m", p=P)
            up_e = a["m_wup"].rearrange("e (k p) m -> p k e m", p=P)
            down_e = a["m_wdown"].rearrange("e m n -> m e n")

            def load_unit(gv, uv, dv, x):
                for n, v in enumerate((gv, uv)):
                    load(e, stage[:, n * D:(n + 1) * D].rearrange("p (k e m) -> p k e m", k=KD, e=1), v[:, :, x, :], "ld_u")
                load(e, stage[:, 2 * D:3 * D].rearrange("p (e n) -> p e n", e=1), dv[:, x, :], "ld_u")

            for u in range(NS):
                wait(e, "unit", u)
                load_unit(gate_s, up_s, down_s, bass.ds(u, 1))
            with e.Fori(0, E) as x:
                wait(e, "unit", x + NS)
                load_unit(gate_e, up_e, down_e, bass.ds(x, 1))

            wait(e, "x1", NT)
            wait(e, "unit", U)
            for c in range(KD):
                load(e, fstage[:, c, :], kp("f_W1")[:, c, :], "ld_f")
            for c in range(2):
                load(e, fstage[:, KD + c, :].rearrange("p (k n) -> p k n", n=D), kp("f_W2")[:, c * 4:c * 4 + 4, :], "ld_f")

            out_v = out.rearrange("(t two) s d -> (two s) t d", two=2)
            def group(g):
                wait(e, "obuf", 2 * g + 2)
                load(e, out_v[:, span(g * TG, TG), :], obuf[:, :, :], "st_out")

            groups(e, group)
            dma_wait(e, "st_out", G)

        @block.gpsimd
        def _(e):
            link = chain(e, "pc")

            def diagonal(t, pattern, base, cm):
                return e.affine_select(out=t, in_=t, compare_op=ALU.not_equal, fill=1.0, base=base,
                                       pattern=pattern, channel_multiplier=cm)

            link(e.memset(ident[:, :], 0.0))
            link(diagonal(ident[:, :], [[-1, P]], 0, 1))
            link(e.memset(half[:, :], -0.5))
            link(e.memset(ones[:, :], 1.0))
            link(e.memset(kblk[:, :, :], 0.0))
            link(e.memset(zeros[:, :], 0.0))
            for t in (vblk_h, vblk_l):
                for par in range(2):
                    link(e.tensor_copy(t[:, par, :, :], zeros[:, :].rearrange("p (b c) -> p b c", b=2)))
            link(e.memset(nvsel[:, :, :], 0.0))
            link(e.memset(wt_raw[:, :, :], 0.0))
            link(e.memset(wgT[:, :], 0.0))
            link(e.memset(relT[:, :], -BIG))
            link(e.iota(col(POS, DH), pattern=[[0, 1]], base=S - 1, channel_multiplier=-1, allow_small_or_imprecise_dtypes=True))
            link(e.iota(decay[:, :], pattern=[[-1, P]], base=-1, channel_multiplier=1, allow_small_or_imprecise_dtypes=True))
            link(e.iota(iota_e[:, :], pattern=[[1, E]], base=0, channel_multiplier=0, allow_small_or_imprecise_dtypes=True))
            link(e.memset(mneg[:, :, :], 0.0), "p_const")
            with nc.allow_non_contiguous_dma(reason="small columns"):
                def column(c, src, lo=0, n=P):
                    load(e, colsc[lo:lo + n, c:c + 1], src, "ld_cols")

                def vec(name):
                    return a[name].rearrange("(p o) -> p o", o=1)

                for k in range(KD):
                    column(GN + k, vec("c_g_norm")[k * P:(k + 1) * P, :])
                    column(GO + k, vec("c_g_out")[k * P:(k + 1) * P, :])
                for lo in (0, DH):
                    column(KSC, vec("c_k_scale"), lo, DH)
                    column(QSC, vec("c_q_scale"), lo, DH)
                    column(NKC, a["cond"][0:1, :].rearrange("o p -> p o"), lo, DH)
                column(DLG, a["t_decay"].to_broadcast([P, 1]))
                column(OSC, a["t_oscale"].to_broadcast([P, 1]))
                for h in range(H):
                    lo = (h % 2) * DH
                    load(e, nvsel[lo:lo + DH, h // 2, h:h + 1], a["cond"][1:2, :].rearrange("o p -> p o"), "ld_null")
                load(e, nkB[:, :], a["cond"][0:1, :].to_broadcast([P, DH]), "ld_null")
                load(e, nullb[:, :], a["c_nullb"].rearrange("(o h) -> o h", o=1).to_broadcast([P, H]), "ld_null")
            wait(e, "v_nss", 1)
            link(e.tensor_tensor(col(NRN), col(NSS), half[:, 0:1], ALU.pow), "p_nrn")
            for n in range(2):
                wait(e, "v_ln", n + 1)
                link(e.tensor_tensor(col(LNR, DH), col(LNV, DH), half[0:DH, 0:1], ALU.pow), "p_ln")
            dma_wait(e, "ld_mask", 2)
            link(e.tensor_scalar(mneg[:, :, 0:S], mask_u[:, :, :], -1.0, BIG, ALU.add, ALU.mult))
            dma_wait(e, "ld_null", H + 2)
            link(e.tensor_copy(bias[:, :, S:NK], nullb[:, :].rearrange("p (h o) -> p h o", o=1)))
            wait(e, "a_decay", 1)
            link(e.affine_select(out=decay[:, :], in_=decay[:, :], compare_op=ALU.is_gt, fill=0.0, base=0,
                                 pattern=[[-1, P]], channel_multiplier=1))
            link(e.memset(decay[S:P, 0:S], 0.0), "p_dec")
            selr = biasm[0:2 * E, :, :].rearrange("p h k -> p (h k)")[:, 0:E * P].rearrange("p (e c) -> p e c", e=E)
            link(e.memset(selr, 0.0))
            link(diagonal(selr, [[-1, E], [0, P]], 0, 1))
            link(diagonal(selr, [[-1, E], [0, P]], -E, 1))
            link(e.tensor_copy(sel[:, :, :], selr), "p_sel")
            wait(e, "v_nkk", 1)
            for b in range(2):
                for r in range(2):
                    last = e.tensor_copy(kblk[r * DH:(r + 1) * DH, b, r * NK + S:r * NK + S + 1],
                                         colsc[r * DH:(r + 1) * DH, NKK:NKK + 1])
            link(last, "p_nkk")
            dma_wait(e, "ld_bias", 2)
            wait(e, "t_nvw", 1)
            wait(e, "t_vo", 1)
            wait(e, "t_mlp", 2)
            wait(e, "v_wout", 1)
            wait(e, "v_rawqkv", 2 * KD)

            def split_unit(u):
                e.wait_ge(sems["ld_u"], 48 * (u + 1))
                dst_h, dst_l = at_tile(wu_h, u), at_tile(wu_l, u)
                done(e.tensor_tensor(dst_h, stage[:, :], ones[:, :].to_broadcast([P, 3 * D]), ALU.mult), "unit_h")
                wait(e, "unit_h", u + 1)
                done(e.tensor_tensor(dst_l, stage[:, :], dst_h.bitcast(F32), ALU.subtract), "unit")
                wait(e, "unit", u + 1)

            for u in range(NS):
                split_unit(u)

            def body(i, par, live):
                if live(0):
                    wait(e, "kT", i + 1)
                    wait(e, "sim_t", NB3 * i)
                    wait(e, "rn", i + 1)
                    for b in range(2):
                        for r in range(2):
                            last = e.tensor_tensor(kblk[r * DH:(r + 1) * DH, b, r * NK:r * NK + S],
                                                   kT[r * DH:(r + 1) * DH, b * S:(b + 1) * S],
                                                   colsc[r * DH:(r + 1) * DH, KQS:KQS + 1].to_broadcast([DH, S]), ALU.mult)
                    done(last, "kblk")
                    wait(e, "kblk", i + 1)
                if live(-2):
                    wait(e, "ln2_ve", i - 1)
                    wait(e, "zn", i - 2)
                    done(e.tensor_tensor(rs2[:, :], ve2[:, :], half[:, 0:1], ALU.pow), "ln2_rs")
                if live(1):
                    wait(e, "sim", i + 1)
                    done(e.tensor_tensor(biasm[:, :, :], bias[:, :, :],
                                         (mneg[:, i + 1:i + 2, :] if isinstance(i, int) else mneg[:, bass.ds(i + 1, 1), :])
                                         .to_broadcast([P, H, NK]), ALU.add), "biasm")
                if live(2):
                    wait(e, "ln1_ve", i + 3)
                    wait(e, "xn", i + 2)
                    done(e.tensor_tensor(rs1[:, :], ve1[:, :], half[:, 0:1], ALU.pow), "ln1_rs")
                if live(1):
                    wait(e, "ss_c", i + 2)
                    wait(e, "qn", i + 1)
                    done(e.tensor_tensor(rn[:, :], sc[:, :], half[:, :], ALU.pow), "rn")

            pipeline(e, body, extra=lambda r: split_unit(r + NS))
            for u in range(NS + PAIRS, U):
                split_unit(u)

            wait(e, "x1", NT)
            def group(g):
                wait(e, "xg", g + 1)
                wait(e, "obuf", 2 * g)
                done(e.tensor_tensor(xb[:, :, :], xg[:, :, :], b2r[:, :].rearrange("p (o d) -> p o d", o=1)
                                     .to_broadcast([P, TG, D]), ALU.add), "xb")
                for u in range(U):
                    wait(e, "hh", U * g + u + 1)
                    done(e.tensor_tensor(hl[:, u % 2, :], hw[:, u % 2, :], hh[:, u % 2, :].bitcast(F32), ALU.subtract), "hl")
                for j in range(FB):
                    wait(e, "fh", FB * g + j + 1)
                    done(e.tensor_tensor(hl[:, j % 2, :], hw[:, j % 2, :], hh[:, j % 2, :].bitcast(F32), ALU.subtract), "fl")

            groups(e, group)

        @block.scalar
        def _(e):
            link = chain(e, "ac")
            wait(e, "v_ln_in", 1)
            link(e.activation(col(EXA), col(ABX), ACT.Exp, scale=-1.0), "a_e1")
            wait(e, "v_neglog", 1)
            link(e.activation(col(LNA), col(EX1), ACT.Ln), "a_e2")
            wait(e, "v_lnd", 1)
            link(e.activation(decay[:, :], decay[:, :], ACT.Exp, scale=col(LND)), "a_decay")
            for n in range(2):
                wait(e, "v_hn", n + 1)
                link(e.activation(h1[:, :], h0[:, :], ACT.Silu), "a_sil")
                if n == 0:
                    for k in range(KD):
                        wait(e, "v_rawqkv", k + 1)
                        link(e.activation(wqkv_h[:, k, :], raw_qkv[:, k, :], ACT.Copy), "a_qkvh")
                    dma_wait(e, "ld_out", 1)
                    link(e.activation(wout_h[:, :, :], raw_out[:, :, :], ACT.Copy), "a_wouth")
            wait(e, "v_wvof", 1)
            link(e.activation(wvo_h[:, :, :], wvo_f[:, :, :], ACT.Copy), "a_wvoh")
            wait(e, "t_nvw", 1)
            link(e.activation(nvw[:, :], bank[6][0:H, 0:D], ACT.Copy), "a_nvw")
            dma_wait(e, "ld_late", KD + 4)
            link(e.activation(wt_h[:, :, :], wt_raw[:, :, :], ACT.Copy), "a_wth")

            def body(i, par, live):
                if live(0):
                    wait(e, "sim_t", NB3 * i)
                    for c in range(2):
                        wait(e, "qT_t", 2 * i + c + 1)
                        done(e.activation(qT[:, 4 * c:4 * c + 4, :], bank[4 + c][:, :].rearrange("p (b t) -> p b t", b=4), ACT.Copy), "qT")
                if live(1):
                    wait(e, "xnT", i + 2)
                    wait(e, "qkv", NB3 * (i + 1))
                    done(e.activation(xnT_h[:, :, :], bank[0][:, 0:D].rearrange("p (k t) -> p k t", k=KD), ACT.Copy), "xnT_h")
                if live(-3):
                    wait(e, "rt_t", i - 2)
                    wait(e, "vo_t", i - 3)
                    done(e.activation(rT_h[:, :, :], bank[7][:, 0:D].rearrange("p (k t) -> p k t", k=KD), ACT.Copy), "rT_h")
                if live(-1):
                    wait(e, "av_t", 2 * (i - 1))
                    for c in range(2):
                        wait(e, "pT_t", 2 * (i - 1) + c + 1)
                        done(e.activation(pT_h[:, 4 * c:4 * c + 4, :], bank[4 + c][:, :].rearrange("p (b t) -> p b t", b=4), ACT.Copy), "pT_h")
                    wait(e, "pnT_t", i)
                    wait(e, "wo_t", i - 1)
                    done(e.activation(pnT[:, :], bank[0][0:H, 0:P], ACT.Copy), "pnT")
                if live(-2):
                    wait(e, "znT_t", i - 1)
                    wait(e, "sc_t", i - 2)
                    done(e.activation(znT[:, :, :], bank[0][:, 0:D].rearrange("p (k t) -> p k t", k=KD), ACT.Copy), "znT")
                if live(0):
                    wait(e, "simc", i + 1)
                    wait(e, "pr", i)
                    done(e.activation(pe[:, :, :], sim[:, :, :], ACT.Exp), "pe")
                if live(1):
                    wait(e, "ss", i + 1)
                    for c in range(NB3):
                        wait(e, "qkv", NB3 * (i + 1) + c + 1)
                        n = min(QH, H + 1 - QH * c)
                        done(e.activation(sq[:, QH * c:QH * c + n, :], bank[1 + c][:, 0:n * DH].rearrange("p (h d) -> p h d", d=DH),
                                          ACT.Square), "sq")
                if live(-1):
                    wait(e, "wo_t", i - 1)
                    for b in range(2):
                        wait(e, "av_t", 2 * (i - 1) + b + 1)
                        done(e.activation(oT_h[:, :, b * S:(b + 1) * S], bank[6 + b][:, :].rearrange("p (c t) -> p c t", c=HP), ACT.Copy), "oT_h")
                if live(1):
                    wait(e, "av_t", 2 * i)
                    wait(e, "qkv", NB3 * (i + 2))
                    for b, r in ((0, 0), (0, 1), (1, 0), (1, 1)):
                        last = e.activation(vblk_h[r * DH:(r + 1) * DH, 1 - par, b, r * DH:(r + 1) * DH],
                                            bank[NB3][b * S:(b + 1) * S, QB - DH:QB], ACT.Copy)
                    done(last, "v_h")
                if live(-2):
                    wait(e, "uT_t", i - 1)
                    done(e.activation(uT[:, :, :], bank[5][:, 0:D].rearrange("p (k t) -> p k t", k=KD), ACT.Copy), "uT")

            pipeline(e, body)

            dma_wait(e, "ld_f", 4)
            for c in range(4):
                dst = w1_h[:, c, :] if c < KD else w2_h[:, (c - KD) * 4:(c - KD) * 4 + 4, :].rearrange("p k n -> p (k n)")
                done(e.activation(dst, fstage[:, c, :], ACT.Copy), "f_h")
            def group(g):
                wait(e, "up_t", U * g)
                for k in range(KD):
                    wait(e, "x1T_t", KD * g + k + 1)
                    done(e.activation(x1T_h[:, k, :], bank[k][:, :], ACT.Copy), "x1T_h")
                for u in range(U):
                    n = U * g + u
                    if u == NS:
                        wait(e, "rv", RV_PER_GROUP * g + RV_EXP)
                        done(e.activation(le[:, :, :], lg[:, :, :], ACT.Exp), "ra")
                        wait(e, "wT_t", g + 1)
                        wait(e, "wb_t", E * g)
                        done(e.activation(wT[:, :], bank[3][0:2 * E, :], ACT.Copy), "wT")
                    wait(e, "gate_t", n + 1)
                    wait(e, "lk", n)
                    done(e.activation(gs[:, :], bank[4 + u % 2][:, :], ACT.Copy), "gs")
                    if u > 0:
                        round_unit(e, g, u - 1)
                round_unit(e, g, U - 1)
                wait(e, "f1_t", FB * g)
                for k in range(KD):
                    wait(e, "down_t", U * g + U)
                    done(e.activation(yT_h[:, k, :], bank[k][:, :], ACT.Copy), "yT_h")
                for j in range(FB):
                    wait(e, "fr", FB * g + j + 1)
                    wait(e, "down_t", U * g + U)
                    if j >= 2:
                        wait(e, "f2_t", FB * g + j - 1)
                    done(e.activation(hh[:, j % 2, :], hw[:, j % 2, :], ACT.Copy), "fh")

            groups(e, group)

        @block.vector
        def _(e):
            link = chain(e, "vc")

            def subtract(dst, full, upper, name):
                done(e.tensor_tensor(dst, full, upper.bitcast(F32), ALU.subtract), name)

            dma_wait(e, "ld_cols", 2 * KD + 8)
            wait(e, "pc", 1)
            wait(e, "p_const", 1)
            link(e.tensor_scalar(col(KQS), col(KSC), col(QSC), 8.0, ALU.mult, ALU.mult))
            for k in range(KD):
                link(e.tensor_tensor(col(GOS + k), col(GO + k), col(OSC), ALU.mult))
            link(e.tensor_scalar(col(NX), col(DLG), -1.0, None, ALU.mult))
            link(e.tensor_scalar(col(MXN), col(NX), 0.0, None, ALU.max))
            link(e.tensor_tensor(col(ABX), col(NX), col(DLG), ALU.max), "v_ln_in")
            wait(e, "a_e1", 1)
            link(e.tensor_scalar(col(EX1), col(EXA), 1.0, None, ALU.add), "v_neglog")
            link(e.tensor_scalar(decay[:, :], decay[:, :], 0.0, None, ALU.max))
            wait(e, "a_e2", 1)
            link(e.tensor_tensor(col(LND), col(LNA), col(MXN), ALU.add))
            link(e.tensor_scalar(col(LND), col(LND), -1.0, None, ALU.mult), "v_lnd")
            dma_wait(e, "ld_null", H + 2)
            link(e.tensor_tensor(nksq[:, :], nkB[:, :], nkB[:, :], ALU.mult))
            link(e.reduce_sum(col(NSS), nksq[:, :], AX_X))
            link(e.tensor_scalar(col(NSS), col(NSS), 1e-24, None, ALU.max), "v_nss")
            wait(e, "p_nrn", 1)
            link(e.tensor_scalar(col(NKK), col(NKC), col(NRN), col(KQS), ALU.mult, ALU.mult), "v_nkk")
            dma_wait(e, "ld_qkv", 2)
            for k in range(KD):
                link(e.tensor_scalar(raw_qkv[:, k, :], raw_qkv[:, k, :], col(GN + k), None, ALU.mult), "v_rawqkv")
            dma_wait(e, "ld_mlp", 8)
            link(e.scalar_tensor_tensor(h0[:, :], rows[:, 0, :], col(POS, DH), rows[:, 1, :], ALU.mult, ALU.add))
            for n in range(2):
                link(e.bn_stats(st6[0:DH, n, :], h0[:, :]))
                link(e.bn_aggr(mv[0:DH, n, :], st6[0:DH, n, :]))
                link(e.tensor_scalar(col(LNV, DH), mv[0:DH, n, 1:2], EPS, None, ALU.add), "v_ln")
                wait(e, "p_ln", n + 1)
                link(e.tensor_scalar(h0[:, :], h0[:, :], mv[0:DH, n, 0:1], col(LNR, DH), ALU.subtract, ALU.mult))
                link(e.tensor_tensor(h0[:, :], h0[:, :], rows[:, 2 + 2 * n, :], ALU.mult), "v_hn")
                wait(e, "t_hT", n + 1)
                link(e.tensor_copy(hT[:, :, :], bank[0][:, 0:2 * DH].rearrange("p (k t) -> p k t", k=KD)), "v_hT")
                wait(e, "t_mlp", n + 1)
                if n == 0:
                    link(e.tensor_tensor(h0[:, :], bank[7][0:DH, 0:D], rows[:, 3, :], ALU.add), "v_lin")
                else:
                    link(e.tensor_tensor(relp[:, :], bank[7][0:DH, 0:H], b2h[:, :], ALU.add), "v_lin")
            wait(e, "t_rel", 1)
            link(e.tensor_copy(relT[:, 0:DH], bank[0][0:H, 0:DH]), "v_rel")
            for k in range(KD):
                wait(e, "a_qkvh", k + 1)
                link(e.tensor_tensor(wqkv_l[:, k, :], raw_qkv[:, k, :], wqkv_h[:, k, :].bitcast(F32), ALU.subtract), "v_rawqkv")
            wait(e, "a_wouth", 1)
            link(e.tensor_tensor(wout_l[:, :, :], raw_out[:, :, :], wout_h[:, :, :].bitcast(F32), ALU.subtract), "v_wout")
            wait(e, "t_woT", 1)
            link(e.tensor_copy(woT[:, :, :], bank[5][:, :].rearrange("p (k n) -> p k n", k=KD)), "v_woT")
            wait(e, "t_mqk", 1)
            for k in range(KD):
                link(e.scalar_tensor_tensor(mqk[:, k, :], bank[1 + k][:, 0:D], col(GO + k), goutr[:, :], ALU.mult, ALU.mult), "v_mqk")
            wait(e, "t_vo", 1)
            link(e.tensor_scalar(wvo_f[:, 0, :], bank[3][:, 0:D], col(GOS), None, ALU.mult))
            link(e.tensor_scalar(wvo_f[:, 1, :], bank[4][:, 0:D], col(GOS + 1), None, ALU.mult), "v_wvof")
            wait(e, "a_wvoh", 1)
            link(e.tensor_tensor(wvo_l[:, :, :], wvo_f[:, :, :], wvo_h[:, :, :].bitcast(F32), ALU.subtract), "v_wvo")
            wait(e, "a_wth", 1)
            link(e.tensor_tensor(wt_l[:, :, :], wt_raw[:, :, :], wt_h[:, :, :].bitcast(F32), ALU.subtract), "v_wtl")

            def layer_norm_stats(src, n, t, st, m, ve_ready, ve, rs_taken):
                done(e.bn_stats(st6[:, n, :], src), st)
                wait(e, st, t + 1)
                settle(e)
                done(e.bn_aggr(mv[:, n, :], st6[:, n, :]), m)
                wait(e, m, t + 1)
                wait(e, rs_taken, t)
                done(e.tensor_scalar(ve[:, :], mv[:, n, 1:2], EPS, None, ALU.add), ve_ready)

            def body(i, par, live):
                if live(0):
                    wait(e, "kT_t", i + 1)
                    wait(e, "kblk", i)
                    done(e.tensor_copy(kT[:, :], bank[0][:, 0:P]), "kT")
                if live(-2):
                    wait(e, "wo_t", i - 1)
                    layer_norm_stats(bank[6][:, 0:D], 1, i - 2, "st2", "mv2", "ln2_ve", ve2, "ln2_rs")
                if live(1):
                    wait(e, "xnT_h", i + 2)
                    subtract(xnT_l[:, :, :], bank[0][:, 0:D].rearrange("p (k t) -> p k t", k=KD), xnT_h[:, :, :], "xnT_l")
                if live(-3):
                    wait(e, "sc_t", i - 2)
                    wait(e, "rt_t", i - 3)
                    done(e.scalar_tensor_tensor(at[:, :], bank[7][:, 0:P], D ** -0.5, decay[:, :], ALU.mult, ALU.mult), "at")
                if live(-2):
                    wait(e, "ln2_rs", i - 1)
                    wait(e, "rt_t", i - 3)
                    done(e.tensor_scalar(zn[:, par, :], bank[6][:, 0:D], mv[:, 1, 0:1], rs2[:, 0:1], ALU.subtract, ALU.mult), "zn")
                if live(0):
                    wait(e, "biasm", i + 1)
                    wait(e, "pe", i)
                    for c in range(NB3):
                        n = min(QH, H - QH * c)
                        wait(e, "sim_t", NB3 * i + c + 1)
                        last = e.tensor_tensor(sim[:, QH * c:QH * c + n, :], bank[1 + c][:, 0:n * NK].rearrange("p (h k) -> p h k", k=NK),
                                               biasm[:, QH * c:QH * c + n, :], ALU.add)
                    done(last, "sim")
                    wait(e, "sim", i + 1)
                    done(e.reduce_max(mx[:, :], sim[:, :, :], AX_X), "mx")
                if live(-3):
                    wait(e, "rT_h", i - 2)
                    subtract(rT_l[:, :, :], bank[7][:, 0:D].rearrange("p (k t) -> p k t", k=KD), rT_h[:, :, :], "rT_l")
                if live(0):
                    wait(e, "mx", i + 1)
                    done(e.tensor_tensor(sim[:, :, :], sim[:, :, :], mx[:, :].rearrange("p (h o) -> p h o", o=1).to_broadcast([P, H, NK]),
                                         ALU.subtract), "simc")
                if live(-1):
                    for c in range(2):
                        wait(e, "pT_h", 2 * (i - 1) + c + 1)
                        subtract(pT_l[:, 4 * c:4 * c + 4, :], bank[4 + c][:, :].rearrange("p (b t) -> p b t", b=4),
                                 pT_h[:, 4 * c:4 * c + 4, :], "pT_l")
                if live(0):
                    wait(e, "pe", i + 1)
                    done(e.reduce_sum(den[:, :], pe[:, :, :], AX_X), "den")
                    wait(e, "den", i + 1)
                    done(e.reciprocal(rden[:, :], den[:, :]), "rden")
                    wait(e, "rden", i + 1)
                    wait(e, "pnT_t", i)
                    for lo, n, dst in ((0, S, pr[:, 0:H * S]), (S, 1, pr[:, H * S:H * NK])):
                        last = e.tensor_tensor(dst.rearrange("p (h k) -> p h k", h=H), pe[:, :, lo:lo + n],
                                               rden[:, :].rearrange("p (h o) -> p h o", o=1).to_broadcast([P, H, n]), ALU.mult)
                    done(last, "pr")
                if live(1):
                    wait(e, "sq", NB3 * (i + 2))
                    done(e.reduce_sum(ss[:, :], sq[:, :, :], AX_X), "ss")
                    wait(e, "ss", i + 2)
                    wait(e, "rn", i + 1)
                    done(e.tensor_scalar(sc[:, :], ss[:, :], 1e-24, None, ALU.max), "ss_c")
                if live(2):
                    if isinstance(i, int) and i + 2 < 4:
                        dma_wait(e, "ld_x0", 1)
                    elif isinstance(i, int):
                        dma_wait(e, "ld_x1", 1)
                    wait(e, "xn", i + 2)
                    layer_norm_stats(at_tile(xs, i + 2), 0, i + 2, "st1", "mv1", "ln1_ve", ve1, "ln1_rs")
                if live(-1):
                    for b in range(2):
                        wait(e, "oT_h", 2 * (i - 1) + b + 1)
                        subtract(oT_l[:, :, b * S:(b + 1) * S], bank[6 + b][:, :].rearrange("p (c t) -> p c t", c=HP),
                                 oT_h[:, :, b * S:(b + 1) * S], "oT_l")
                if live(1):
                    wait(e, "rn", i + 2)
                    wait(e, "kT_t", i + 1)
                    wait(e, "v_h", i + 2)
                    done(e.tensor_scalar(kn2[:, :, :], bank[NB3][:, QB - 2 * DH:QB - DH].rearrange("p (o d) -> p o d", o=1).to_broadcast([P, 2, DH]),
                                         rn[:, H:H + 1], None, ALU.mult), "kn2")
                    wait(e, "qT_t", 2 * (i + 1))
                    for c in range(NB3):
                        n = min(QH, H - QH * c)
                        last = e.tensor_tensor(qn[:, QH * c:QH * c + n, :], bank[1 + c][:, 0:n * DH].rearrange("p (h d) -> p h d", d=DH),
                                               rn[:, QH * c:QH * c + n].rearrange("p (h o) -> p h o", o=1).to_broadcast([P, n, DH]), ALU.mult)
                    done(last, "qn")
                    wait(e, "v_h", i + 2)
                    for b, r in ((0, 0), (0, 1), (1, 0), (1, 1)):
                        at_b = (slice(r * DH, (r + 1) * DH), 1 - par, b, slice(r * DH, (r + 1) * DH))
                        last = e.tensor_tensor(vblk_l[at_b], bank[NB3][b * S:(b + 1) * S, QB - DH:QB], vblk_h[at_b].bitcast(F32), ALU.subtract)
                    done(last, "vblk")
                if live(-3):
                    wait(e, "vo_t", i - 2)
                    done(e.tensor_tensor(at_tile(xs, i - 3), bank[4][:, 0:D], at_tile(xs, i - 3), ALU.add), "x1")
                if live(2):
                    wait(e, "ln1_rs", i + 3)
                    wait(e, "xnT", i + 2)
                    done(e.tensor_scalar(xn[:, :], at_tile(xs, i + 2), mv[:, 0, 0:1], rs1[:, 0:1], ALU.subtract, ALU.mult), "xn")

            pipeline(e, body)

            wait(e, "x1", NT)
            for c in range(4):
                wait(e, "f_h", c + 1)
                pick = (lambda w1, w2: w1[:, c, :] if c < KD else w2[:, (c - KD) * 4:(c - KD) * 4 + 4, :].rearrange("p k n -> p (k n)"))
                subtract(pick(w1_l, w2_l), fstage[:, c, :], pick(w1_h, w2_h), "f_l")

            def group(g):
                wait(e, "x1T_t", KD * g)
                wait(e, "xb", g)
                done(e.tensor_copy(xg[:, :, :], xs[:, span(g * TG, TG), :]), "xg")
                for k in range(KD):
                    wait(e, "x1T_h", KD * g + k + 1)
                    subtract(x1T_l[:, k, :], bank[k][:, :], x1T_h[:, k, :], "x1T_l")
                wait(e, "lg_t", g + 1)
                done(e.tensor_scalar(lgT[:, :], bank[2][0:E, :], 0.5, None, ALU.mult), "lgT")

                def unit(u):
                    n = U * g + u
                    par = u % 2
                    wait(e, "gs", n + 1)
                    wait(e, "hw", n)
                    done(e.scalar_tensor_tensor(lk[:, :], gs[:, :], 0.01, gs[:, :], ALU.mult, ALU.max), "lk")
                    wait(e, "lk", n + 1)
                    wait(e, "up_t", n + 1)
                    if u >= 2:
                        wait(e, "hl", n - 1)
                    else:
                        wait(e, "hl", n)
                        wait(e, "fl", FB * g)
                    if u < NS:
                        done(e.tensor_tensor(hw[:, par, :], lk[:, :], bank[6 + par][:, :], ALU.mult), "hw")
                    else:
                        done(e.tensor_tensor(hu[:, :], lk[:, :], bank[6 + par][:, :], ALU.mult), "hu")
                        wait(e, "hu", E * g + u - NS + 1)
                        wait(e, "wb_t", E * g + u - NS + 1)
                        done(e.tensor_tensor(hw[:, par, :], hu[:, :], bank[2][:, :], ALU.mult), "hw")

                for u in range(NS):
                    unit(u)

                step = [0]

                def rlink(ins):
                    step[0] += 1
                    done(ins, "rv")
                    wait(e, "rv", RV_PER_GROUP * g + step[0])

                def over_experts(t):
                    return t[:, :].rearrange("p (t o) -> p t o", o=1).to_broadcast([P, TG, E])

                wait(e, "lgtr", g + 1)
                rlink(e.tensor_copy(lg[:, :, :], bank[3][:, 0:TG * E].rearrange("p (t e) -> p t e", e=E)))
                rlink(e.reduce_max(lmax[:, :], lg[:, :, :], AX_X))
                rlink(e.tensor_tensor(lg[:, :, :], lg[:, :, :], over_experts(lmax), ALU.subtract))
                assert step[0] == RV_EXP
                wait(e, "ra", g + 1)
                rlink(e.reduce_sum(lsum[:, :], le[:, :, :], AX_X))
                rlink(e.reciprocal(lrec[:, :], lsum[:, :]))
                rlink(e.tensor_tensor(score[:, :, :], le[:, :, :], over_experts(lrec), ALU.mult))
                settle(e)
                for t in range(TG):
                    last = e.max(top[:, t, :], score[:, t, :])
                rlink(last)
                settle(e)
                for t in range(TG):
                    last = e.max_index(topi[:, t, :], top[:, t, :], score[:, t, :])
                rlink(last)
                rlink(e.tensor_copy(topf[:, :, :], topi[:, :, :]))
                rlink(e.reduce_sum(tsum[:, :], top[:, :, 0:2], AX_X))
                rlink(e.tensor_scalar(tsum[:, :], tsum[:, :], 1e-20, None, ALU.add))
                rlink(e.reciprocal(trec[:, :], tsum[:, :]))
                rlink(e.tensor_tensor(topw[:, :, :], top[:, :, 0:2], trec[:, :].rearrange("p (t o) -> p t o", o=1).to_broadcast([P, TG, 2]), ALU.mult))
                for r in range(2):
                    for t in range(TG):
                        last = (e.tensor_scalar(wk[:, r, t, :], iota_e[:, :], topf[:, t, r:r + 1], topw[:, t, r:r + 1], ALU.is_equal, ALU.mult))
                rlink(last)
                rlink(e.tensor_tensor(wf[:, :, :], wk[:, 0, :, :], wk[:, 1, :, :], ALU.add))
                rlink(e.tensor_copy(wr[:, :, :], wf[:, :, :]))
                wait(e, "wT_t", g)
                rlink(e.tensor_copy(wst[:, :, 0:E], wr[:, :, :].bitcast(F32)))
                done(e.tensor_tensor(wst[:, :, E:2 * E], wf[:, :, :], wr[:, :, :].bitcast(F32), ALU.subtract), "wst")
                assert step[0] == RV_PER_GROUP

                for u in range(NS, U):
                    unit(u)
                for k in range(KD):
                    wait(e, "yT_h", KD * g + k + 1)
                    subtract(yT_l[:, k, :], bank[k][:, :], yT_h[:, k, :], "yT_l")
                for j in range(FB):
                    wait(e, "f1_t", FB * g + j + 1)
                    if j >= 2:
                        wait(e, "fl", FB * g + j - 1)
                    else:
                        wait(e, "hl", U * g + U)
                    done(e.tensor_scalar(hw[:, j % 2, :], bank[4 + j % 2][:, :], b1c[:, j:j + 1], 0.0, ALU.add, ALU.max), "fr")
                wait(e, "f2_t", FB * g + FB)
                wait(e, "xb", g + 1)
                wait(e, "st_out", 16 * g)
                for c in range(2):
                    done(e.tensor_tensor(obuf[:, 2 * c:2 * c + 2, :], bank[6 + c][:, :].rearrange("p (t n) -> p t n", t=2),
                                         xb[:, 2 * c:2 * c + 2, :], ALU.add), "obuf")

            groups(e, group)

        @block.tensor
        def _(e):
            wait(e, "p_const", 1)
            dma_wait(e, "ld_mlp", 8)
            for n in range(2):
                wait(e, "a_sil", n + 1)
                for k in range(KD):
                    last = e.transpose(bank[0][:, k * DH:(k + 1) * DH], h1[:, k * P:(k + 1) * P], ident[0:DH, 0:DH])
                done(last, "t_hT")
                wait(e, "v_hT", n + 1)
                for k in range(KD):
                    last = e.matmul(bank[7][0:DH, 0:(D, H)[n]], hT[:, k, :], (raw_w1, w2p)[n][:, k, :], start=k == 0, stop=k == KD - 1)
                done(last, "t_mlp")
            wait(e, "v_lin", 2)
            done(e.transpose(bank[0][0:H, 0:DH], relp[:, :], ident[0:DH, 0:DH]), "t_rel")
            dma_wait(e, "ld_att", 5)
            for k in range(KD):
                for j in range(KD):
                    last = e.transpose(bank[5][:, k * D + j * P:k * D + (j + 1) * P], raw_att[:, 3, j, k * P:(k + 1) * P], ident[:, :])
            done(last, "t_woT")
            for i in range(KD):
                for k in range(KD):
                    last = e.matmul(bank[1 + i][:, 0:D], raw_att[:, 0, k, i * P:(i + 1) * P], raw_att[:, 1, k, :], start=k == 0, stop=k == KD - 1)
            done(last, "t_mqk")
            wait(e, "v_woT", 1)
            for i in range(KD):
                for k in range(KD):
                    last = e.matmul(bank[3 + i][:, 0:D], raw_att[:, 2, k, i * P:(i + 1) * P], woT[:, k, :], start=k == 0, stop=k == KD - 1)
            done(last, "t_vo")
            dma_wait(e, "ld_null", H + 2)
            dma_wait(e, "ld_out", 1)
            for c in range(HP):
                last = e.matmul(bank[6][0:H, 0:D], nvsel[:, c, :], raw_out[:, c, :], start=c == 0, stop=c == HP - 1)
            done(last, "t_nvw")
            wait(e, "v_wvof", 1)
            wait(e, "v_mqk", KD)
            wait(e, "a_nvw", 1)
            wait(e, "v_rel", 1)

            def body(i, par, live):
                if live(0):
                    wait(e, "kn2", i + 1)
                    wait(e, "znT", i - 2)
                    done(e.transpose(bank[0][:, 0:P], kn2[:, :, :].rearrange("p a d -> p (a d)"), ident[:, :]), "kT_t")
                    wait(e, "qn", i + 1)
                    wait(e, "x1", i - 3)
                    wait(e, "uT", i - 2)
                    for c in range(2):
                        for j in range(4):
                            h = 8 * c + 2 * j
                            last = e.transpose(bank[4 + c][:, j * P:(j + 1) * P], qn[:, h:h + 2, :].rearrange("p h d -> p (h d)"), ident[:, :])
                        done(last, "qT_t")
                if live(-2):
                    wait(e, "oT_l", 2 * (i - 1))
                    wait(e, "pnT", i - 1)
                    for c in range(HP):
                        split_passes(e, bank[6][:, 0:D], (oT_h[:, c, :], oT_l[:, c, :]), (wout_h[:, c, :], wout_l[:, c, :]), c == 0, False)
                    done(e.matmul(bank[6][:, 0:D], pnT[:, :], nvw[:, :], start=False, stop=True), "wo_t")
                if live(1):
                    wait(e, "xn", i + 2)
                    wait(e, "kT", i + 1)
                    for k in range(KD):
                        last = e.transpose(bank[0][:, k * P:(k + 1) * P], xn[:, k * P:(k + 1) * P], ident[:, :])
                    done(last, "xnT")
                if live(-3):
                    wait(e, "uT", i - 2)
                    wait(e, "oT_l", 2 * (i - 1) if live(-2) else 2 * NT)
                    for k in range(KD):
                        last = e.matmul(bank[7][:, 0:P], znT[:, k, :], uT[:, k, :], start=k == 0, stop=k == KD - 1)
                    done(last, "sc_t")
                if live(0):
                    wait(e, "kblk", i + 1)
                    wait(e, "qT", 2 * (i + 1))
                    wait(e, "vblk", i + 1)
                    for c in range(HP):
                        for b in range(2):
                            last = e.matmul(bank[1 + c // PB][b * S:(b + 1) * S, (c % PB) * 2 * NK:(c % PB + 1) * 2 * NK],
                                            qT[:, c, b * S:(b + 1) * S], kblk[:, b, :], start=True, stop=True)
                        if c % PB == PB - 1 or c == HP - 1:
                            done(last, "sim_t")
                if live(-3):
                    wait(e, "at", i - 2)
                    for k in range(KD):
                        last = e.matmul(bank[7][:, k * P:(k + 1) * P], zn[:, 1 - par, k * P:(k + 1) * P], at[:, :], start=True, stop=True)
                    done(last, "rt_t")
                if live(-1):
                    wait(e, "pr", i)
                    wait(e, "qT", 2 * (i + 1) if live(0) else 2 * NT)
                    wait(e, "xnT_l", i + 2 if live(1) else NT)
                    for c in range(2):
                        for j in range(4):
                            h = 8 * c + 2 * j
                            last = e.transpose(bank[4 + c][:, j * P:(j + 1) * P], pr[:, h * S:(h + 2) * S], ident[:, :])
                        done(last, "pT_t")
                    done(e.transpose(bank[0][0:H, 0:P], pr[:, H * S:H * NK], ident[:, :]), "pnT_t")
                if live(1):
                    wait(e, "xnT_l", i + 2)
                    wait(e, "sim", i + 1)
                    for c in range(NB3):
                        for k in range(KD):
                            last = split_passes(e, bank[1 + c][:, 0:QB], (xnT_h[:, k, :], xnT_l[:, k, :]),
                                                (wqkv_h[:, k, c * QB:(c + 1) * QB], wqkv_l[:, k, c * QB:(c + 1) * QB]), k == 0, k == KD - 1)
                        done(last, "qkv")
                if live(-2):
                    wait(e, "zn", i - 1)
                    wait(e, "pnT", i if live(-1) else NT)
                    wait(e, "xnT_l", i + 2 if live(1) else NT)
                    for k in range(KD):
                        last = e.transpose(bank[0][:, k * P:(k + 1) * P], zn[:, par, k * P:(k + 1) * P], ident[:, :])
                    done(last, "znT_t")
                if live(-1):
                    wait(e, "pT_l", 2 * i)
                    wait(e, "vblk", i)
                    wait(e, "zn", i - 1)
                    wait(e, "rT_l", i - 2)
                    for b in range(2):
                        last = split_passes(e, bank[6 + b][:, :], (vblk_h[:, 1 - par, b, :], vblk_l[:, 1 - par, b, :]),
                                            (pT_h[:, :, b * S:(b + 1) * S], pT_l[:, :, b * S:(b + 1) * S]), True, True)
                        done(last, "av_t")
                if live(-3):
                    wait(e, "rT_l", i - 2)
                    wait(e, "pT_l", 2 * i if live(-1) else 2 * NT)
                    for k in range(KD):
                        last = split_passes(e, bank[4][:, 0:D], (rT_h[:, k, :], rT_l[:, k, :]), (wvo_h[:, k, :], wvo_l[:, k, :]), k == 0, k == KD - 1)
                    done(last, "vo_t")
                if live(-2):
                    wait(e, "znT", i - 1)
                    wait(e, "pT_l", 2 * i if live(-1) else 2 * NT)
                    for j in range(KD):
                        for k in range(KD):
                            last = e.matmul(bank[5][:, j * P:(j + 1) * P], mqk[:, k, j * P:(j + 1) * P], znT[:, k, :], start=k == 0, stop=k == KD - 1)
                    done(last, "uT_t")

            wait(e, "v_wvo", 1)
            wait(e, "v_wout", 1)
            wait(e, "p_dec", 1)
            wait(e, "p_nkk", 1)
            pipeline(e, body)

            wait(e, "unit", U)
            wait(e, "p_sel", 1)
            wait(e, "v_wtl", 1)
            wait(e, "x1", NT)
            def group(g):
                wait(e, "xg", g + 1)
                wait(e, "yT_l", KD * g)
                for k in range(KD):
                    for t in range(TG):
                        last = e.transpose(bank[k][:, t * P:(t + 1) * P], xg[:, t, k * P:(k + 1) * P], ident[:, :])
                    done(last, "x1T_t")
                wait(e, "x1T_l", KD * (g + 1))
                x_parts = [(x1T_h[:, k, :], x1T_l[:, k, :]) for k in range(KD)]
                wait(e, "hw", U * g)
                for k in range(KD):
                    split_passes(e, bank[2][:, :], (wt_h[:, k, :], wt_l[:, k, :]), x_parts[k], k == 0, False)
                done(e.matmul(bank[2][:, :], wgT[:, :], condT[:, span(g * SB, SB)].rearrange("c (s o) -> c s o", o=1).to_broadcast([DH, SB, S]),
                              start=False, stop=True), "lg_t")

                def gate_up(u):
                    n = U * g + u
                    par = u % 2
                    if u < 2:
                        wait(e, "fr", FB * g)
                        wait(e, "obuf", 2 * g)
                    else:
                        wait(e, "gs", n - 1)
                        if u - 2 < NS:
                            wait(e, "hw", n - 1)
                        else:
                            wait(e, "hu", E * g + u - 2 - NS + 1)
                    for o, name, b in ((0, "gate_t", 4), (D, "up_t", 6)):
                        for k in range(KD):
                            w = slice(o + k * M, o + (k + 1) * M)
                            last = split_passes(e, bank[b + par][:, :], (wu_h[:, u, w], wu_l[:, u, w]), x_parts[k], k == 0, k == KD - 1)
                        done(last, name)

                def down(u):
                    wait(e, "hl", U * g + u + 1)
                    for k in range(KD):
                        w = slice(2 * D + k * P, 2 * D + (k + 1) * P)
                        last = split_passes(e, bank[k][:, :], (wu_h[:, u, w], wu_l[:, u, w]), (hh[:, u % 2, :], hl[:, u % 2, :]), u == 0, u == U - 1)
                    done(last, "down_t")

                def spread(u):
                    wait(e, "hw", U * g + u)
                    done(e.matmul(bank[2][:, :], sel[:, u - NS, :], wT[:, :], start=True, stop=True), "wb_t")

                gate_up(0)
                wait(e, "lgT", g + 1)
                wait(e, "wT", g)
                for t in range(TG):
                    last = e.matmul(bank[3][:, t * E:(t + 1) * E], lgT[:, t * P:(t + 1) * P], ident[0:E, 0:E], start=True, stop=True)
                done(last, "lgtr")
                for u in range(1, U + 1):
                    if u < U:
                        gate_up(u)
                    if u == NS:
                        wait(e, "wst", g + 1)
                        for t in range(TG):
                            last = e.transpose(bank[3][0:2 * E, t * P:(t + 1) * P], wst[:, t, :], ident[:, :])
                        done(last, "wT_t")
                        wait(e, "wT", g + 1)
                    if NS <= u < U:
                        spread(u)
                    down(u - 1)

                y_parts = [(yT_h[:, k, :], yT_l[:, k, :]) for k in range(KD)]
                wait(e, "yT_l", KD * (g + 1))
                wait(e, "f_l", 4)

                def second(j):
                    wait(e, "fl", FB * g + j + 1)
                    for t in range(TG):
                        last = split_passes(e, bank[6 + t // 2][:, (t % 2) * D:(t % 2 + 1) * D],
                                            (hh[:, j % 2, t * P:(t + 1) * P], hl[:, j % 2, t * P:(t + 1) * P]),
                                            (w2_h[:, j, :], w2_l[:, j, :]), j == 0 and t % 2 == 0, j == FB - 1, skip_group_check=True)
                    done(last, "f2_t")

                for j in range(FB + 1):
                    if j < FB:
                        if j >= 2:
                            wait(e, "fr", FB * g + j - 1)
                        for k in range(KD):
                            last = split_passes(e, bank[4 + j % 2][:, :], (w1_h[:, k, j * P:(j + 1) * P], w1_l[:, k, j * P:(j + 1) * P]),
                                                y_parts[k], k == 0, k == KD - 1)
                        done(last, "f1_t")
                    if j > 0:
                        second(j - 1)

            groups(e, group)


_SHORT = {
    "x": "x", "cond": "cond_64", "mask": "mask_BxS_bf1",
    "c_g_norm": "L0_cond_g_norm", "c_Wq": "L0_cond_Wq", "c_Wkv": "L0_cond_Wkv", "c_q_scale": "L0_cond_q_scale",
    "c_k_scale": "L0_cond_k_scale", "c_nullb": "L0_cond_null_attn_bias", "c_w0": "L0_cond_w0", "c_b0": "L0_cond_b0",
    "c_g0": "L0_cond_g0", "c_w1": "L0_cond_w1", "c_b1": "L0_cond_b1", "c_g1": "L0_cond_g1", "c_w2": "L0_cond_w2",
    "c_b2": "L0_cond_b2", "c_Wout": "L0_cond_Wout", "c_g_out": "L0_cond_g_out",
    "t_Wq": "L0_attn_Wq", "t_Wk": "L0_attn_Wk", "t_Wv": "L0_attn_Wv", "t_Wo": "L0_attn_Wo",
    "t_decay": "L0_attn_decay_logit", "t_oscale": "L0_attn_out_scale",
    "m_wt": "L0_cond2_wt", "m_wg": "L0_cond2_wg", "m_wgate": "L0_cond2_w_gate", "m_wup": "L0_cond2_w_up",
    "m_wdown": "L0_cond2_w_down", "m_sg": "L0_cond2_sw_gate", "m_su": "L0_cond2_sw_up", "m_sd": "L0_cond2_sw_down",
    "f_W1": "L0_ffn_W1", "f_b1": "L0_ffn_b1", "f_W2": "L0_ffn_W2", "f_b2": "L0_ffn_b2",
}


def kernel(**inputs):
    import numpy as np
    import concourse.bacc as bacc
    from concourse.bass_utils import run_bass_kernel_spmd

    nc = bacc.Bacc("TRN2", target_bir_lowering=False, num_devices=1)
    arrays, aps = {}, {}
    for short, name in _SHORT.items():
        v = np.ascontiguousarray(inputs[name])
        if v.ndim == 0 or short in ("t_decay", "t_oscale"):
            v = v.reshape(1, 1)
        if v.dtype == np.bool_:
            v = v.view(np.uint8)
        arrays["in_" + short] = v
        aps[short] = nc.dram_tensor("in_" + short, v.shape, mybir.dt.from_np(v.dtype), kind="ExternalInput").ap()
    out = nc.dram_tensor("out", (B, S, D), F32, kind="ExternalOutput").ap()
    adaln_attention_ffn(nc, aps, out)
    r = run_bass_kernel_spmd(nc, [arrays], core_ids=[0])
    return r.results[0]["out"]
```

```python
import concourse.bass as bass
from concourse import mybir
from contextlib import ExitStack

F32 = mybir.dt.float32
F32R = mybir.dt.float32r
U32 = mybir.dt.uint32
U8 = mybir.dt.uint8
ALU = mybir.AluOpType
ACT = mybir.ActivationFunctionType
AX_X = mybir.AxisListType.X

P = 128
B, S, D = 32, 64, 256
T = B * S
NT = T // P
KD = D // P
H, DH = 16, 64
HP = H // 2
NK = S + 1
QKV = H * DH + 2 * DH
NB3 = 3
QB = QKV // NB3
QH = QB // DH
PB = QH // 2
E, M = 8, 128
NS = 2
U = NS + E
INTER = 1024
FB = INTER // P
G = 4
GT = T // G
TG = GT // P
SB = GT // S
BIG = 1.5e38
EPS = 1e-5
BANK = 512



def adaln_attention_ffn(nc, a, out):
    ctx = ExitStack()
    with ctx:
        def sb(name, shape, dt=F32, scope=ctx):
            return scope.enter_context(nc.sbuf_tensor(name, shape, dt))

        xs = sb("xs", [P, NT, D])
        ident = sb("ident", [P, P])
        wu_h = sb("wu_h", [P, U, 3 * D], F32R)
        wt_h = sb("wt_h", [P, KD, P], F32R)
        wt_l = sb("wt_l", [P, KD, P], F32R)
        wgT = sb("wgT", [DH, P])
        condT = sb("condT", [DH, B])
        sel = sb("sel", [2 * E, E, P], F32R)
        iota_e = sb("iota_e", [P, E])
        b1c = sb("b1c", [P, FB])
        b2r = sb("b2r", [P, D])
        carrier = sb("carrier", [P, 1])

        with ExitStack() as early:
            raw_qkv = sb("raw_qkv", [P, KD, QKV], scope=early)
            raw_out = sb("raw_out", [P, HP, D], scope=early)
            raw_att = sb("raw_att", [P, 4, KD, D], scope=early)
            raw_w1 = sb("raw_w1", [P, KD, D], scope=early)
            woT = sb("woT", [P, KD, D], scope=early)
        wu_l = sb("wu_l", [P, U, 3 * D], F32R)

        with ExitStack() as first:
            def s1(name, shape, dt=F32):
                return sb(name, shape, dt, first)
            stage = s1("stage", [P, 3 * D])
            wqkv_h = s1("wqkv_h", [P, KD, QKV], F32R)
            wqkv_l = s1("wqkv_l", [P, KD, QKV], F32R)
            wout_h = s1("wout_h", [P, HP, D], F32R)
            wout_l = s1("wout_l", [P, HP, D], F32R)
            mqk = s1("mqk", [P, KD, D])
            wvo_h = s1("wvo_h", [P, KD, D], F32R)
            wvo_l = s1("wvo_l", [P, KD, D], F32R)
            nvw = s1("nvw", [H, D])
            nvsel = s1("nvsel", [P, HP, H])
            bias = s1("bias", [P, H, NK])
            biasm = s1("biasm", [P, H, NK])
            mneg = s1("mneg", [P, NT, NK])
            decay = s1("decay", [P, P])
            colsc = s1("colsc", [P, 32])
            ones = s1("ones", [P, 1])
            half = s1("half", [P, H + 1])
            st6 = s1("st6", [P, 2, 6])
            mv = s1("mv", [P, 2, 2])
            ve1 = s1("ve1", [P, 1])
            ve2 = s1("ve2", [P, 1])
            rs1 = s1("rs1", [P, 1])
            rs2 = s1("rs2", [P, 1])
            xn = s1("xn", [P, D])
            xnT_h = s1("xnT_h", [P, KD, P], F32R)
            xnT_l = s1("xnT_l", [P, KD, P], F32R)
            sq = s1("sq", [P, H + 1, DH])
            ss = s1("ss", [P, H + 1])
            sc = s1("sc", [P, H + 1])
            rn = s1("rn", [P, H + 1])
            qn = s1("qn", [P, H, DH])
            kn2 = s1("kn2", [P, 2, DH])
            qT = s1("qT", [P, HP, P])
            kT = s1("kT", [P, P])
            kblk = s1("kblk", [P, 2, 2 * NK])
            vblk_h = s1("vblk_h", [P, 2, 2, P], F32R)
            vblk_l = s1("vblk_l", [P, 2, 2, P], F32R)
            sim = s1("sim", [P, H, NK])
            mx = s1("mx", [P, H])
            pe = s1("pe", [P, H, NK])
            den = s1("den", [P, H])
            rden = s1("rden", [P, H])
            pr = s1("pr", [P, H * NK])
            pnT = s1("pnT", [H, P])
            zn = s1("zn", [P, 2, D])
            znT = s1("znT", [P, KD, P])
            uT = s1("uT", [P, KD, P])
            at = s1("at", [P, P])
            rT_h = s1("rT_h", [P, KD, P], F32R)
            rT_l = s1("rT_l", [P, KD, P], F32R)
            with ExitStack() as early2:
                def s2(name, shape, dt=F32):
                    return sb(name, shape, dt, early2)
                rows = s2("rows", [DH, 5, D])
                h0 = s2("h0", [DH, D])
                h1 = s2("h1", [DH, D])
                hT = s2("hT", [P, KD, DH])
                w2p = s2("w2p", [P, KD, H])
                b2h = s2("b2h", [DH, H])
                relp = s2("relp", [DH, H])
                relT = s2("relT", [H, 2 * DH])
                goutr = s2("goutr", [P, D])
                wvo_f = s2("wvo_f", [P, KD, D])
                wt_raw = s2("wt_raw", [P, KD, P])
                nkB = s2("nkB", [P, DH])
                nksq = s2("nksq", [P, DH])
                nullb = s2("nullb", [P, H])
                mask_u = s2("mask_u", [P, NT, S], U8)
                zeros = s2("zeros", [P, 2 * P])
            pT_h = s1("pT_h", [P, HP, P], F32R)
            pT_l = s1("pT_l", [P, HP, P], F32R)
            oT_h = s1("oT_h", [P, HP, P], F32R)
            oT_l = s1("oT_l", [P, HP, P], F32R)

        w1_h = sb("w1_h", [P, KD, INTER], F32R)
        w1_l = sb("w1_l", [P, KD, INTER], F32R)
        w2_h = sb("w2_h", [P, FB, D], F32R)
        w2_l = sb("w2_l", [P, FB, D], F32R)
        fstage = sb("fstage", [P, 4, 2 * BANK])
        xg = sb("xg", [P, TG, D])
        xb = sb("xb", [P, TG, D])
        x1T_h = sb("x1T_h", [P, KD, GT], F32R)
        x1T_l = sb("x1T_l", [P, KD, GT], F32R)
        lgT = sb("lgT", [E, GT])
        lg = sb("lg", [P, TG, E])
        lmax = sb("lmax", [P, TG])
        le = sb("le", [P, TG, E])
        lsum = sb("lsum", [P, TG])
        lrec = sb("lrec", [P, TG])
        score = sb("score", [P, TG, E])
        top = sb("top", [P, TG, 8])
        topi = sb("topi", [P, TG, 8], U32)
        topf = sb("topf", [P, TG, 8])
        tsum = sb("tsum", [P, TG])
        trec = sb("trec", [P, TG])
        topw = sb("topw", [P, TG, 2])
        wk = sb("wk", [P, 2, TG, E])
        wf = sb("wf", [P, TG, E])
        wr = sb("wr", [P, TG, E], F32R)
        wst = sb("wst", [P, TG, 2 * E])
        wT = sb("wT", [2 * E, GT], F32R)
        gs = sb("gs", [P, GT])
        lk = sb("lk", [P, GT])
        hu = sb("hu", [P, GT])
        hw = sb("hw", [P, 2, GT])
        hh = sb("hh", [P, 2, GT], F32R)
        hl = sb("hl", [P, 2, GT], F32R)
        yT_h = sb("yT_h", [P, KD, GT], F32R)
        yT_l = sb("yT_l", [P, KD, GT], F32R)
        obuf = sb("obuf", [P, TG, D])

        bank = [ctx.enter_context(nc.psum_tensor(f"bank{i}", [P, BANK], F32)) for i in range(8)]
        rel_dram = nc.dram_tensor("rel_scratch", (H, S, S), F32, kind="Internal")

        sems = {}
        for n in """ld_x0 ld_x1 ld_qkv ld_out ld_att ld_mlp ld_cols ld_mask ld_null ld_late st_rel ld_bias ld_u ld_f st_out
                    pc vc ac p_const p_nrn p_ln p_dec p_nkk p_bias p_mneg p_sel v_nss v_nkk v_ln v_hn v_hT v_rel
                    v_exp v_rawqkv v_wout v_mqk v_wvof v_wvo v_neglog v_ln_in v_lnd v_lin
                    a_sil a_qkvh a_wouth a_wvoh a_e1 a_e2 a_decay a_nvw a_wth v_wtl
                    t_hT t_mlp t_woT t_mqk t_vo t_nvw t_rel v_woT unit_h unit
                    st1 mv1 ln1_ve ln1_rs xn xnT xnT_h xnT_l qkv sq ss ss_c rn qn kn2 v_h
                    kT_t kT kblk vblk qT_t qT sim_t biasm sim mx simc pe den rden pr
                    pT_t pT_h pT_l pnT_t pnT av_t oT_h oT_l wo_t st2 mv2 ln2_ve ln2_rs zn
                    znT_t znT uT_t uT sc_t at rt_t rT_h rT_l vo_t x1
                    f_h f_l xg xb x1T_t x1T_h x1T_l f2_c lg_t lgT lgtr rv ra wst wT_t wT
                    gate_t up_t wb_t gs lk hu hw hh hl down_t yT_h yT_l f1_t fr fh fl f2_t obuf""".split():
            sems[n] = ctx.enter_context(nc.semaphore("s_" + n))

        def wait(e, name, count):
            if not isinstance(count, int) or count > 0:
                e.wait_ge(sems[name], count)

        def settle(e):
            e.memset(carrier[:, :], 0.0)

        def dma_wait(e, name, n):
            e.wait_ge(sems[name], 16 * n)

        def done(ins, name):
            ins.then_inc(sems[name], 1)

        def load(e, dst, src, name):
            e.dma_start(dst, src).then_inc(sems[name], 16)

        def chain(e, own):
            counts = {}

            def link(ins, name=own):
                counts[name] = counts.get(name, 0) + 1
                done(ins, name)
                e.wait_ge(sems[name], counts[name])
            return link

        GN, GO, KSC, QSC, DLG, OSC, NKC, NSS, NRN, KQS, LNV, LNR, POS, GOS, NKK, NX, MXN, ABX, EXA, LNA, LND, EX1 = (
            0, 2, 4, 5, 6, 7, 8, 9, 10, 11, 12, 13, 14, 15, 17, 18, 19, 20, 21, 22, 23, 24)

        def col(c, n=P):
            return colsc[0:n, c:c + 1]

        FIRST_I, LAST_I = -2, NT + 2
        STEADY0, STEADY1 = 4, NT - 3
        PAIRS = (STEADY1 - STEADY0 + 1) // 2
        SPLIT0 = 2

        def pipeline(e, body):
            def edge(i):
                body(i, i % 2, lambda off: 0 <= i + off < NT, divmod(i - SPLIT0, 2) if SPLIT0 <= i < SPLIT0 + 2 * E else None)
            for i in range(FIRST_I, STEADY0):
                edge(i)
            with e.Fori(0, PAIRS) as r:
                for half_step in range(2):
                    body(2 * r + (STEADY0 + half_step), (STEADY0 + half_step) % 2, lambda off: True, (r + (STEADY0 - SPLIT0) // 2, half_step))
            for i in range(STEADY0 + 2 * PAIRS, LAST_I + 1):
                edge(i)

        def groups(e, body):
            body(0, True)
            with e.Fori(1, G - 1) as g:
                body(g, True)
            body(G - 1, False)

        def span(lo, n):
            return slice(lo, lo + n) if isinstance(lo, int) else bass.ds(lo, n)

        def at_tile(t3, i):
            if isinstance(i, int):
                return t3[:, i, :]
            return t3[:, bass.ds(i, 1), :].rearrange("p o d -> p (o d)")

        def split_passes(e, dst, stat, mov, start, stop, **kw):
            e.matmul(dst, stat[0], mov[0], start=start, stop=False, **kw)
            e.matmul(dst, stat[0], mov[1], start=False, stop=False, **kw)
            return e.matmul(dst, stat[1], mov[0], start=False, stop=stop, **kw)

        RV_EXP = 3
        RV_PER_GROUP = RV_EXP + 14
        DENSE_AT = (3, 5, 7, 9)

        def round_unit(e, g, u):
            n, par = U * g + u, u % 2
            wait(e, "hw", n + 1)
            if u >= 2:
                wait(e, "down_t", n - 1)
            wait(e, "f2_c", 2 * g)
            done(e.activation(hh[:, par, :], hw[:, par, :], ACT.Copy), "hh")

        block = ctx.enter_context(nc.Block())

        @block.sync
        def _(e):
            x_v = a["x"].rearrange("(t two) s d -> (two s) t d", two=2)

            def kp(name):
                return a[name].rearrange("(k p) n -> p k n", p=P)

            def row(name, n):
                return a[name].rearrange("(o d) -> o d", o=1).to_broadcast([n, a[name].shape[0]])

            load(e, xs[:, 0:4, :], x_v[:, 0:4, :], "ld_x0")
            load(e, raw_qkv[:, :, 0:H * DH], kp("c_Wq"), "ld_qkv")
            load(e, raw_qkv[:, :, H * DH:QKV], kp("c_Wkv"), "ld_qkv")
            load(e, rows[:, 0, :], a["c_w0"].to_broadcast([DH, D]), "ld_mlp")
            for n, name in enumerate(("c_b0", "c_g0", "c_b1", "c_g1")):
                load(e, rows[:, 1 + n, :], row(name, DH), "ld_mlp")
            load(e, raw_w1[:, :, :], kp("c_w1"), "ld_mlp")
            load(e, w2p[:, :, :], kp("c_w2"), "ld_mlp")
            load(e, b2h[:, :], row("c_b2", DH), "ld_mlp")
            mask_v = a["mask"].rearrange("(t two) s -> two t s", two=2)
            for b in range(2):
                load(e, mask_u[b * S:(b + 1) * S, :, :], mask_v[b:b + 1, :, :].to_broadcast([S, NT, S]), "ld_mask")
            load(e, raw_out[:, :, :], kp("c_Wout"), "ld_out")
            for n, name in enumerate(("t_Wq", "t_Wk", "t_Wv", "t_Wo")):
                load(e, raw_att[:, n, :, :], kp(name), "ld_att")
            load(e, goutr[:, :], row("c_g_out", P), "ld_att")
            load(e, xs[:, 4:NT, :], x_v[:, 4:NT, :], "ld_x1")
            wait(e, "p_const", 1)
            with nc.allow_non_contiguous_dma(reason="small transposed tables"):
                for k in range(KD):
                    load(e, wt_raw[:, k, 0:E], a["m_wt"][:, k * P:(k + 1) * P].rearrange("e p -> p e"), "ld_late")
                load(e, wgT[:, 0:E], a["m_wg"].rearrange("e g -> g e"), "ld_late")
                load(e, condT[:, :], a["cond"].rearrange("b g -> g b"), "ld_late")
                load(e, b1c[:, :], a["f_b1"].rearrange("(j p) -> p j", p=P), "ld_late")
            load(e, b2r[:, :], row("f_b2", P), "ld_late")
            wait(e, "v_rel", 1)
            ladder = relT[:, S - 1:2 * S - 1]
            ladder = bass.AP(tensor=ladder.tensor, offset=ladder.offset, ap=[ladder.ap[0], [-1, S], [1, S]])
            load(e, rel_dram.ap(), ladder, "st_rel")
            dma_wait(e, "st_rel", 1)
            for b in range(2):
                load(e, bias[b * S:(b + 1) * S, :, 0:S],
                     rel_dram.ap().rearrange("h i j -> i h j"), "ld_bias")

            gate_s = a["m_sg"].rearrange("(k p) (u m) -> p k u m", p=P, m=M)
            up_s = a["m_su"].rearrange("(k p) (u m) -> p k u m", p=P, m=M)
            down_s = a["m_sd"].rearrange("(u m) n -> m u n", m=M)
            gate_e = a["m_wgate"].rearrange("e (k p) m -> p k e m", p=P)
            up_e = a["m_wup"].rearrange("e (k p) m -> p k e m", p=P)
            down_e = a["m_wdown"].rearrange("e m n -> m e n")

            def load_unit(gv, uv, dv, x):
                for n, v in enumerate((gv, uv)):
                    load(e, stage[:, n * D:(n + 1) * D].rearrange("p (k e m) -> p k e m", k=KD, e=1), v[:, :, x, :], "ld_u")
                load(e, stage[:, 2 * D:3 * D].rearrange("p (e n) -> p e n", e=1), dv[:, x, :], "ld_u")

            for u in range(NS):
                wait(e, "unit", u)
                load_unit(gate_s, up_s, down_s, bass.ds(u, 1))
            with e.Fori(0, E) as x:
                wait(e, "unit", x + NS)
                load_unit(gate_e, up_e, down_e, bass.ds(x, 1))

            wait(e, "x1", NT)
            wait(e, "unit", U)
            for c in range(KD):
                load(e, fstage[:, c, :], kp("f_W1")[:, c, :], "ld_f")
            for c in range(2):
                load(e, fstage[:, KD + c, :].rearrange("p (k n) -> p k n", n=D), kp("f_W2")[:, c * 4:c * 4 + 4, :], "ld_f")

            out_v = out.rearrange("(t two) s d -> (two s) t d", two=2)
            def group(g, more):
                wait(e, "obuf", 2 * g + 2)
                load(e, out_v[:, span(g * TG, TG), :], obuf[:, :, :], "st_out")

            groups(e, group)
            dma_wait(e, "st_out", G)

        @block.gpsimd
        def _(e):
            link = chain(e, "pc")

            def diagonal(t, pattern, base, cm):
                return e.affine_select(out=t, in_=t, compare_op=ALU.not_equal, fill=1.0, base=base,
                                       pattern=pattern, channel_multiplier=cm)

            link(e.memset(ident[:, :], 0.0))
            link(diagonal(ident[:, :], [[-1, P]], 0, 1))
            link(e.memset(half[:, :], -0.5))
            link(e.memset(ones[:, :], 1.0))
            link(e.memset(kblk[:, :, :], 0.0))
            link(e.memset(zeros[:, :], 0.0))
            for t in (vblk_h, vblk_l):
                for par in range(2):
                    link(e.tensor_copy(t[:, par, :, :], zeros[:, :].rearrange("p (b c) -> p b c", b=2)))
            link(e.memset(nvsel[:, :, :], 0.0))
            link(e.memset(wt_raw[:, :, :], 0.0))
            link(e.memset(wgT[:, :], 0.0))
            link(e.memset(relT[:, :], -BIG))
            link(e.iota(col(POS, DH), pattern=[[0, 1]], base=S - 1, channel_multiplier=-1, allow_small_or_imprecise_dtypes=True))
            link(e.iota(decay[:, :], pattern=[[-1, P]], base=-1, channel_multiplier=1, allow_small_or_imprecise_dtypes=True))
            link(e.iota(iota_e[:, :], pattern=[[1, E]], base=0, channel_multiplier=0, allow_small_or_imprecise_dtypes=True))
            link(e.memset(mneg[:, :, :], 0.0), "p_const")
            with nc.allow_non_contiguous_dma(reason="small columns"):
                def column(c, src, lo=0, n=P):
                    load(e, colsc[lo:lo + n, c:c + 1], src, "ld_cols")

                def vec(name):
                    return a[name].rearrange("(p o) -> p o", o=1)

                for k in range(KD):
                    column(GN + k, vec("c_g_norm")[k * P:(k + 1) * P, :])
                    column(GO + k, vec("c_g_out")[k * P:(k + 1) * P, :])
                for lo in (0, DH):
                    column(KSC, vec("c_k_scale"), lo, DH)
                    column(QSC, vec("c_q_scale"), lo, DH)
                    column(NKC, a["cond"][0:1, :].rearrange("o p -> p o"), lo, DH)
                column(DLG, a["t_decay"].to_broadcast([P, 1]))
                column(OSC, a["t_oscale"].to_broadcast([P, 1]))
                for h in range(H):
                    lo = (h % 2) * DH
                    load(e, nvsel[lo:lo + DH, h // 2, h:h + 1], a["cond"][1:2, :].rearrange("o p -> p o"), "ld_null")
                load(e, nkB[:, :], a["cond"][0:1, :].to_broadcast([P, DH]), "ld_null")
                load(e, nullb[:, :], a["c_nullb"].rearrange("(o h) -> o h", o=1).to_broadcast([P, H]), "ld_null")
            wait(e, "v_nss", 1)
            link(e.tensor_tensor(col(NRN), col(NSS), half[:, 0:1], ALU.pow), "p_nrn")
            for n in range(2):
                wait(e, "v_ln", n + 1)
                link(e.tensor_tensor(col(LNR, DH), col(LNV, DH), half[0:DH, 0:1], ALU.pow), "p_ln")
            dma_wait(e, "ld_mask", 2)
            link(e.tensor_scalar(mneg[:, :, 0:S], mask_u[:, :, :], -1.0, BIG, ALU.add, ALU.mult))
            dma_wait(e, "ld_null", H + 2)
            link(e.tensor_copy(bias[:, :, S:NK], nullb[:, :].rearrange("p (h o) -> p h o", o=1)))
            wait(e, "a_decay", 1)
            link(e.affine_select(out=decay[:, :], in_=decay[:, :], compare_op=ALU.is_gt, fill=0.0, base=0,
                                 pattern=[[-1, P]], channel_multiplier=1))
            link(e.memset(decay[S:P, 0:S], 0.0), "p_dec")
            selr = biasm[0:2 * E, :, :].rearrange("p h k -> p (h k)")[:, 0:E * P].rearrange("p (e c) -> p e c", e=E)
            link(e.memset(selr, 0.0))
            link(diagonal(selr, [[-1, E], [0, P]], 0, 1))
            link(diagonal(selr, [[-1, E], [0, P]], -E, 1))
            link(e.tensor_copy(sel[:, :, :], selr), "p_sel")
            wait(e, "v_nkk", 1)
            for b in range(2):
                for r in range(2):
                    last = e.tensor_copy(kblk[r * DH:(r + 1) * DH, b, r * NK + S:r * NK + S + 1],
                                         colsc[r * DH:(r + 1) * DH, NKK:NKK + 1])
            link(last, "p_nkk")
            dma_wait(e, "ld_bias", 2)
            wait(e, "t_nvw", 1)
            wait(e, "t_vo", 1)
            wait(e, "t_mlp", 2)
            wait(e, "v_wout", 1)
            wait(e, "v_rawqkv", 2 * KD)

            def split_unit(u, part):
                if part == 0:
                    e.wait_ge(sems["ld_u"], 48 * (u + 1))
                    done(e.tensor_tensor(at_tile(wu_h, u), stage[:, :], ones[:, :].to_broadcast([P, 3 * D]), ALU.mult), "unit_h")
                else:
                    wait(e, "unit_h", u + 1)
                    done(e.tensor_tensor(at_tile(wu_l, u), stage[:, :], at_tile(wu_h, u).bitcast(F32), ALU.subtract), "unit")

            for u in range(NS):
                split_unit(u, 0)
                split_unit(u, 1)

            def body(i, par, live, part):
                if live(0):
                    wait(e, "kT", i + 1)
                    wait(e, "sim_t", NB3 * i)
                    wait(e, "rn", i + 1)
                    wait(e, "pr", i)
                    for r in range(2):
                        head = slice(r * DH, (r + 1) * DH)
                        last = e.tensor_tensor(kblk[head, :, r * NK:r * NK + S], kT[head, :].rearrange("p (b s) -> p b s", b=2),
                                               colsc[head, KQS:KQS + 1].rearrange("p (o s) -> p o s", o=1).to_broadcast([DH, 2, S]), ALU.mult)
                    done(last, "kblk")
                    wait(e, "kblk", i + 1)
                if live(-2):
                    wait(e, "ln2_ve", i - 1)
                    wait(e, "zn", i - 2)
                    done(e.tensor_tensor(rs2[:, :], ve2[:, :], half[:, 0:1], ALU.pow), "ln2_rs")
                if live(1):
                    wait(e, "sim", NB3 * (i + 1))
                    done(e.tensor_tensor(biasm[:, :, :], bias[:, :, :],
                                         (mneg[:, i + 1:i + 2, :] if isinstance(i, int) else mneg[:, bass.ds(i + 1, 1), :])
                                         .to_broadcast([P, H, NK]), ALU.add), "biasm")
                if part is not None:
                    split_unit(part[0] + NS, part[1])
                if live(1):
                    wait(e, "ss_c", i + 2)
                    wait(e, "qn", i + 1)
                    done(e.tensor_tensor(rn[:, :], sc[:, :], half[:, :], ALU.pow), "rn")

                if live(2):
                    wait(e, "ln1_ve", i + 3)
                    wait(e, "xn", i + 2)
                    done(e.tensor_tensor(rs1[:, :], ve1[:, :], half[:, 0:1], ALU.pow), "ln1_rs")
                if live(0):
                    wait(e, "rden", i + 1)
                    wait(e, "pnT_t", i)
                    for lo, n, dst in ((0, S, pr[:, 0:H * S]), (S, 1, pr[:, H * S:H * NK])):
                        last = e.tensor_tensor(dst.rearrange("p (h k) -> p h k", h=H), pe[:, :, lo:lo + n],
                                               rden[:, :].rearrange("p (h o) -> p h o", o=1).to_broadcast([P, H, n]), ALU.mult)
                    done(last, "pr")

            pipeline(e, body)

            wait(e, "x1", NT)
            wait(e, "unit", U)
            def group(g, more):
                wait(e, "obuf", 2 * g)
                done(e.tensor_tensor(xb[:, :, :], xs[:, span(g * TG, TG), :], b2r[:, :].rearrange("p (o d) -> p o d", o=1)
                                     .to_broadcast([P, TG, D]), ALU.add), "xb")
                for u in range(U):
                    wait(e, "hh", U * g + u + 1)
                    done(e.tensor_tensor(hl[:, u % 2, :], hw[:, u % 2, :], hh[:, u % 2, :].bitcast(F32), ALU.subtract), "hl")
                for j in range(FB):
                    wait(e, "fh", FB * g + j + 1)
                    done(e.tensor_tensor(hl[:, j % 2, :], hw[:, j % 2, :], hh[:, j % 2, :].bitcast(F32), ALU.subtract), "fl")

            groups(e, group)

        @block.scalar
        def _(e):
            link = chain(e, "ac")
            wait(e, "v_ln_in", 1)
            link(e.activation(col(EXA), col(ABX), ACT.Exp, scale=-1.0), "a_e1")
            wait(e, "v_neglog", 1)
            link(e.activation(col(LNA), col(EX1), ACT.Ln), "a_e2")
            wait(e, "v_lnd", 1)
            link(e.activation(decay[:, :], decay[:, :], ACT.Exp, scale=col(LND)), "a_decay")
            for n in range(2):
                wait(e, "v_hn", n + 1)
                link(e.activation(h1[:, :], h0[:, :], ACT.Silu), "a_sil")
                if n == 0:
                    for k in range(KD):
                        wait(e, "v_rawqkv", k + 1)
                        link(e.activation(wqkv_h[:, k, :], raw_qkv[:, k, :], ACT.Copy), "a_qkvh")
                    dma_wait(e, "ld_out", 1)
                    link(e.activation(wout_h[:, :, :], raw_out[:, :, :], ACT.Copy), "a_wouth")
            wait(e, "v_wvof", 1)
            link(e.activation(wvo_h[:, :, :], wvo_f[:, :, :], ACT.Copy), "a_wvoh")
            wait(e, "t_nvw", 1)
            link(e.activation(nvw[:, :], bank[6][0:H, 0:D], ACT.Copy), "a_nvw")
            dma_wait(e, "ld_late", KD + 4)
            link(e.activation(wt_h[:, :, :], wt_raw[:, :, :], ACT.Copy), "a_wth")

            def body(i, par, live, part):
                if live(0):
                    wait(e, "sim_t", NB3 * i)
                    for c in range(2):
                        wait(e, "qT_t", 2 * i + c + 1)
                        done(e.activation(qT[:, 4 * c:4 * c + 4, :], bank[4 + c][:, :].rearrange("p (b t) -> p b t", b=4), ACT.Copy), "qT")
                if live(1):
                    wait(e, "xnT", i + 2)
                    wait(e, "qkv", NB3 * (i + 1))
                    done(e.activation(xnT_h[:, :, :], bank[0][:, 0:D].rearrange("p (k t) -> p k t", k=KD), ACT.Copy), "xnT_h")
                if live(-3):
                    wait(e, "rt_t", i - 2)
                    wait(e, "vo_t", i - 3)
                    done(e.activation(rT_h[:, :, :], bank[7][:, 0:D].rearrange("p (k t) -> p k t", k=KD), ACT.Copy), "rT_h")
                if live(-1):
                    wait(e, "av_t", 2 * (i - 1))
                    for c in range(2):
                        wait(e, "pT_t", 2 * (i - 1) + c + 1)
                        done(e.activation(pT_h[:, 4 * c:4 * c + 4, :], bank[4 + c][:, :].rearrange("p (b t) -> p b t", b=4), ACT.Copy), "pT_h")
                    wait(e, "pnT_t", i)
                    wait(e, "wo_t", i - 1)
                    done(e.activation(pnT[:, :], bank[0][0:H, 0:P], ACT.Copy), "pnT")
                def squares(c):
                    if c == 0:
                        wait(e, "ss", i + 1)
                    wait(e, "qkv", NB3 * (i + 1) + c + 1)
                    n = min(QH, H + 1 - QH * c)
                    done(e.activation(sq[:, QH * c:QH * c + n, :], bank[1 + c][:, 0:n * DH].rearrange("p (h d) -> p h d", d=DH),
                                      ACT.Square), "sq")

                if live(1):
                    for c in range(NB3 - 1):
                        squares(c)
                if live(0):
                    wait(e, "simc", i + 1)
                    wait(e, "pr", i)
                    done(e.activation(pe[:, :, :], sim[:, :, :], ACT.Exp), "pe")
                if live(1):
                    squares(NB3 - 1)
                if live(-1):
                    wait(e, "wo_t", i - 1)
                    for b in range(2):
                        wait(e, "av_t", 2 * (i - 1) + b + 1)
                        done(e.activation(oT_h[:, :, b * S:(b + 1) * S], bank[6 + b][:, :].rearrange("p (c t) -> p c t", c=HP), ACT.Copy), "oT_h")
                if live(-2):
                    wait(e, "znT_t", i - 1)
                    wait(e, "sc_t", i - 2)
                    done(e.activation(znT[:, :, :], bank[0][:, 0:D].rearrange("p (k t) -> p k t", k=KD), ACT.Copy), "znT")
                if live(1):
                    wait(e, "av_t", 2 * i)
                    wait(e, "qkv", NB3 * (i + 2))
                    for b, r in ((0, 0), (0, 1), (1, 0), (1, 1)):
                        last = e.activation(vblk_h[r * DH:(r + 1) * DH, 1 - par, b, r * DH:(r + 1) * DH],
                                            bank[NB3][b * S:(b + 1) * S, QB - DH:QB], ACT.Copy)
                    done(last, "v_h")
                if live(-2):
                    wait(e, "uT_t", i - 1)
                    done(e.activation(uT[:, :, :], bank[5][:, 0:D].rearrange("p (k t) -> p k t", k=KD), ACT.Copy), "uT")

            pipeline(e, body)

            wait(e, "x1", NT)
            wait(e, "unit", U)

            def split_dense(c):
                dma_wait(e, "ld_f", 4)
                dst = w1_h[:, c, :] if c < KD else w2_h[:, (c - KD) * 4:(c - KD) * 4 + 4, :].rearrange("p k n -> p (k n)")
                done(e.activation(dst, fstage[:, c, :], ACT.Copy), "f_h")

            def x_upper(g, k):
                wait(e, "up_t", U * g)
                wait(e, "x1T_t", KD * g + k + 1)
                done(e.activation(x1T_h[:, k, :], bank[4 + k][:, :], ACT.Copy), "x1T_h")

            def router_exp(g):
                wait(e, "rv", RV_PER_GROUP * g + RV_EXP)
                done(e.activation(le[:, :, :], lg[:, :, :], ACT.Exp), "ra")

            def router_weights(g):
                wait(e, "wT_t", g + 1)
                wait(e, "wb_t", E * g)
                done(e.activation(wT[:, :], bank[3][0:2 * E, :], ACT.Copy), "wT")

            for k in range(KD):
                x_upper(0, k)
            router_exp(0)
            router_weights(0)

            def group(g, more):
                for u in range(U):
                    n = U * g + u
                    wait(e, "gate_t", n + 1)
                    wait(e, "lk", n)
                    done(e.activation(gs[:, :], bank[4 + u % 2][:, :], ACT.Copy), "gs")
                    if u == U - 1 and more:
                        x_upper(g + 1, 0)
                    round_unit(e, g, u)
                    if u == U - 1 and more:
                        x_upper(g + 1, 1)
                    if isinstance(g, int) and g == 0 and u in DENSE_AT:
                        split_dense(DENSE_AT.index(u))
                wait(e, "f1_t", FB * g)
                for k in range(KD):
                    wait(e, "down_t", U * g + U)
                    done(e.activation(yT_h[:, k, :], bank[k][:, :], ACT.Copy), "yT_h")
                for j in range(FB):
                    wait(e, "fr", FB * g + j + 1)
                    wait(e, "down_t", U * g + U)
                    if j >= 2:
                        wait(e, "f2_t", (FB - 1) * g + j - 1)
                    done(e.activation(hh[:, j % 2, :], hw[:, j % 2, :], ACT.Copy), "fh")
                    if j == 1 and more:
                        router_exp(g + 1)
                if more:
                    router_weights(g + 1)

            groups(e, group)

        @block.vector
        def _(e):
            link = chain(e, "vc")

            def subtract(dst, full, upper, name):
                done(e.tensor_tensor(dst, full, upper.bitcast(F32), ALU.subtract), name)

            dma_wait(e, "ld_cols", 2 * KD + 8)
            wait(e, "pc", 1)
            wait(e, "p_const", 1)
            link(e.tensor_scalar(col(KQS), col(KSC), col(QSC), 8.0, ALU.mult, ALU.mult))
            for k in range(KD):
                link(e.tensor_tensor(col(GOS + k), col(GO + k), col(OSC), ALU.mult))
            link(e.tensor_scalar(col(NX), col(DLG), -1.0, None, ALU.mult))
            link(e.tensor_scalar(col(MXN), col(NX), 0.0, None, ALU.max))
            link(e.tensor_tensor(col(ABX), col(NX), col(DLG), ALU.max), "v_ln_in")
            wait(e, "a_e1", 1)
            link(e.tensor_scalar(col(EX1), col(EXA), 1.0, None, ALU.add), "v_neglog")
            link(e.tensor_scalar(decay[:, :], decay[:, :], 0.0, None, ALU.max))
            wait(e, "a_e2", 1)
            link(e.tensor_tensor(col(LND), col(LNA), col(MXN), ALU.add))
            link(e.tensor_scalar(col(LND), col(LND), -1.0, None, ALU.mult), "v_lnd")
            dma_wait(e, "ld_null", H + 2)
            link(e.tensor_tensor(nksq[:, :], nkB[:, :], nkB[:, :], ALU.mult))
            link(e.reduce_sum(col(NSS), nksq[:, :], AX_X))
            link(e.tensor_scalar(col(NSS), col(NSS), 1e-24, None, ALU.max), "v_nss")
            wait(e, "p_nrn", 1)
            link(e.tensor_scalar(col(NKK), col(NKC), col(NRN), col(KQS), ALU.mult, ALU.mult), "v_nkk")
            dma_wait(e, "ld_qkv", 2)
            for k in range(KD):
                link(e.tensor_scalar(raw_qkv[:, k, :], raw_qkv[:, k, :], col(GN + k), None, ALU.mult), "v_rawqkv")
            dma_wait(e, "ld_mlp", 8)
            link(e.scalar_tensor_tensor(h0[:, :], rows[:, 0, :], col(POS, DH), rows[:, 1, :], ALU.mult, ALU.add))
            for n in range(2):
                link(e.bn_stats(st6[0:DH, n, :], h0[:, :]))
                link(e.bn_aggr(mv[0:DH, n, :], st6[0:DH, n, :]))
                link(e.tensor_scalar(col(LNV, DH), mv[0:DH, n, 1:2], EPS, None, ALU.add), "v_ln")
                wait(e, "p_ln", n + 1)
                link(e.tensor_scalar(h0[:, :], h0[:, :], mv[0:DH, n, 0:1], col(LNR, DH), ALU.subtract, ALU.mult))
                link(e.tensor_tensor(h0[:, :], h0[:, :], rows[:, 2 + 2 * n, :], ALU.mult), "v_hn")
                wait(e, "t_hT", n + 1)
                link(e.tensor_copy(hT[:, :, :], bank[0][:, 0:2 * DH].rearrange("p (k t) -> p k t", k=KD)), "v_hT")
                wait(e, "t_mlp", n + 1)
                if n == 0:
                    link(e.tensor_tensor(h0[:, :], bank[7][0:DH, 0:D], rows[:, 3, :], ALU.add), "v_lin")
                else:
                    link(e.tensor_tensor(relp[:, :], bank[7][0:DH, 0:H], b2h[:, :], ALU.add), "v_lin")
            wait(e, "t_rel", 1)
            link(e.tensor_copy(relT[:, 0:DH], bank[0][0:H, 0:DH]), "v_rel")
            for k in range(KD):
                wait(e, "a_qkvh", k + 1)
                link(e.tensor_tensor(wqkv_l[:, k, :], raw_qkv[:, k, :], wqkv_h[:, k, :].bitcast(F32), ALU.subtract), "v_rawqkv")
            wait(e, "a_wouth", 1)
            link(e.tensor_tensor(wout_l[:, :, :], raw_out[:, :, :], wout_h[:, :, :].bitcast(F32), ALU.subtract), "v_wout")
            wait(e, "t_woT", 1)
            link(e.tensor_copy(woT[:, :, :], bank[5][:, :].rearrange("p (k n) -> p k n", k=KD)), "v_woT")
            wait(e, "t_mqk", 1)
            for k in range(KD):
                link(e.scalar_tensor_tensor(mqk[:, k, :], bank[1 + k][:, 0:D], col(GO + k), goutr[:, :], ALU.mult, ALU.mult), "v_mqk")
            wait(e, "t_vo", 1)
            link(e.tensor_scalar(wvo_f[:, 0, :], bank[3][:, 0:D], col(GOS), None, ALU.mult))
            link(e.tensor_scalar(wvo_f[:, 1, :], bank[4][:, 0:D], col(GOS + 1), None, ALU.mult), "v_wvof")
            wait(e, "a_wvoh", 1)
            link(e.tensor_tensor(wvo_l[:, :, :], wvo_f[:, :, :], wvo_h[:, :, :].bitcast(F32), ALU.subtract), "v_wvo")
            wait(e, "a_wth", 1)
            link(e.tensor_tensor(wt_l[:, :, :], wt_raw[:, :, :], wt_h[:, :, :].bitcast(F32), ALU.subtract), "v_wtl")

            def layer_norm_stats(src, n, t, st, m, ve_ready, ve, rs_taken):
                done(e.bn_stats(st6[:, n, :], src), st)
                wait(e, st, t + 1)
                settle(e)
                done(e.bn_aggr(mv[:, n, :], st6[:, n, :]), m)
                wait(e, m, t + 1)
                wait(e, rs_taken, t)
                done(e.tensor_scalar(ve[:, :], mv[:, n, 1:2], EPS, None, ALU.add), ve_ready)

            def body(i, par, live, part):
                if live(0):
                    wait(e, "kT_t", i + 1)
                    wait(e, "kblk", i)
                    done(e.tensor_copy(kT[:, :], bank[0][:, 0:P]), "kT")
                if live(-2):
                    wait(e, "wo_t", i - 1)
                    layer_norm_stats(bank[6][:, 0:D], 1, i - 2, "st2", "mv2", "ln2_ve", ve2, "ln2_rs")
                if live(1):
                    wait(e, "xnT_h", i + 2)
                    subtract(xnT_l[:, :, :], bank[0][:, 0:D].rearrange("p (k t) -> p k t", k=KD), xnT_h[:, :, :], "xnT_l")
                if live(-3):
                    wait(e, "sc_t", i - 2)
                    wait(e, "rt_t", i - 3)
                    done(e.scalar_tensor_tensor(at[:, :], bank[7][:, 0:P], D ** -0.5, decay[:, :], ALU.mult, ALU.mult), "at")
                if live(-2):
                    wait(e, "ln2_rs", i - 1)
                    wait(e, "rt_t", i - 3)
                    done(e.tensor_scalar(zn[:, par, :], bank[6][:, 0:D], mv[:, 1, 0:1], rs2[:, 0:1], ALU.subtract, ALU.mult), "zn")
                if live(0):
                    wait(e, "biasm", i + 1)
                    wait(e, "pe", i)
                    for c in range(NB3):
                        n = min(QH, H - QH * c)
                        wait(e, "sim_t", NB3 * i + c + 1)
                        done(e.tensor_tensor(sim[:, QH * c:QH * c + n, :], bank[1 + c][:, 0:n * NK].rearrange("p (h k) -> p h k", k=NK),
                                               biasm[:, QH * c:QH * c + n, :], ALU.add), "sim")
                    wait(e, "sim", NB3 * (i + 1))
                    done(e.reduce_max(mx[:, :], sim[:, :, :], AX_X), "mx")
                if live(-3):
                    wait(e, "rT_h", i - 2)
                    subtract(rT_l[:, :, :], bank[7][:, 0:D].rearrange("p (k t) -> p k t", k=KD), rT_h[:, :, :], "rT_l")
                if live(0):
                    wait(e, "mx", i + 1)
                    done(e.tensor_tensor(sim[:, :, :], sim[:, :, :], mx[:, :].rearrange("p (h o) -> p h o", o=1).to_broadcast([P, H, NK]),
                                         ALU.subtract), "simc")
                if live(-1):
                    for c in range(2):
                        wait(e, "pT_h", 2 * (i - 1) + c + 1)
                        subtract(pT_l[:, 4 * c:4 * c + 4, :], bank[4 + c][:, :].rearrange("p (b t) -> p b t", b=4),
                                 pT_h[:, 4 * c:4 * c + 4, :], "pT_l")
                if live(1):
                    wait(e, "sq", NB3 * (i + 2))
                    done(e.reduce_sum(ss[:, :], sq[:, :, :], AX_X), "ss")
                    wait(e, "ss", i + 2)
                    wait(e, "rn", i + 1)
                    done(e.tensor_scalar(sc[:, :], ss[:, :], 1e-24, None, ALU.max), "ss_c")
                if live(-1):
                    for b in range(2):
                        wait(e, "oT_h", 2 * (i - 1) + b + 1)
                        subtract(oT_l[:, :, b * S:(b + 1) * S], bank[6 + b][:, :].rearrange("p (c t) -> p c t", c=HP),
                                 oT_h[:, :, b * S:(b + 1) * S], "oT_l")
                if live(0):
                    wait(e, "pe", i + 1)
                    done(e.reduce_sum(den[:, :], pe[:, :, :], AX_X), "den")
                    wait(e, "den", i + 1)
                    wait(e, "pr", i)
                    done(e.reciprocal(rden[:, :], den[:, :]), "rden")
                if live(-3):
                    wait(e, "vo_t", i - 2)
                    done(e.tensor_tensor(at_tile(xs, i - 3), bank[4][:, 0:D], at_tile(xs, i - 3), ALU.add), "x1")
                if live(2):
                    if isinstance(i, int) and i + 2 < 4:
                        dma_wait(e, "ld_x0", 1)
                    elif isinstance(i, int):
                        dma_wait(e, "ld_x1", 1)
                    wait(e, "xn", i + 2)
                    layer_norm_stats(at_tile(xs, i + 2), 0, i + 2, "st1", "mv1", "ln1_ve", ve1, "ln1_rs")
                if live(1):
                    wait(e, "rn", i + 2)
                    wait(e, "kT_t", i + 1)
                    wait(e, "v_h", i + 2)
                    done(e.tensor_scalar(kn2[:, :, :], bank[NB3][:, QB - 2 * DH:QB - DH].rearrange("p (o d) -> p o d", o=1).to_broadcast([P, 2, DH]),
                                         rn[:, H:H + 1], None, ALU.mult), "kn2")
                    wait(e, "qT_t", 2 * (i + 1))
                    for c in range(NB3):
                        n = min(QH, H - QH * c)
                        last = e.tensor_tensor(qn[:, QH * c:QH * c + n, :], bank[1 + c][:, 0:n * DH].rearrange("p (h d) -> p h d", d=DH),
                                               rn[:, QH * c:QH * c + n].rearrange("p (h o) -> p h o", o=1).to_broadcast([P, n, DH]), ALU.mult)
                    done(last, "qn")
                    wait(e, "v_h", i + 2)
                    for b, r in ((0, 0), (0, 1), (1, 0), (1, 1)):
                        at_b = (slice(r * DH, (r + 1) * DH), 1 - par, b, slice(r * DH, (r + 1) * DH))
                        last = e.tensor_tensor(vblk_l[at_b], bank[NB3][b * S:(b + 1) * S, QB - DH:QB], vblk_h[at_b].bitcast(F32), ALU.subtract)
                    done(last, "vblk")
                if live(2):
                    wait(e, "ln1_rs", i + 3)
                    wait(e, "xnT", i + 2)
                    done(e.tensor_scalar(xn[:, :], at_tile(xs, i + 2), mv[:, 0, 0:1], rs1[:, 0:1], ALU.subtract, ALU.mult), "xn")

            pipeline(e, body)

            wait(e, "x1", NT)
            wait(e, "unit", U)

            def split_dense(c):
                wait(e, "f_h", c + 1)
                pick = (lambda w1, w2: w1[:, c, :] if c < KD else w2[:, (c - KD) * 4:(c - KD) * 4 + 4, :].rearrange("p k n -> p (k n)"))
                subtract(pick(w1_l, w2_l), fstage[:, c, :], pick(w1_h, w2_h), "f_l")

            def tokens(g):
                wait(e, "x1T_t", KD * g)
                done(e.tensor_copy(xg[:, :, :], xs[:, span(g * TG, TG), :]), "xg")

            def x_lower(g):
                for k in range(KD):
                    wait(e, "x1T_h", KD * g + k + 1)
                    subtract(x1T_l[:, k, :], bank[4 + k][:, :], x1T_h[:, k, :], "x1T_l")

            def logits(g):
                wait(e, "lg_t", g + 1)
                done(e.tensor_scalar(lgT[:, :], bank[3][0:E, :], 0.5, None, ALU.mult), "lgT")

            def router(g):
                step = [0]

                def rlink(ins):
                    step[0] += 1
                    done(ins, "rv")
                    wait(e, "rv", RV_PER_GROUP * g + step[0])

                def over_experts(t):
                    return t[:, :].rearrange("p (t o) -> p t o", o=1).to_broadcast([P, TG, E])

                wait(e, "lgtr", g + 1)
                rlink(e.tensor_copy(lg[:, :, :], bank[2][:, 0:TG * E].rearrange("p (t e) -> p t e", e=E)))
                rlink(e.reduce_max(lmax[:, :], lg[:, :, :], AX_X))
                rlink(e.tensor_tensor(lg[:, :, :], lg[:, :, :], over_experts(lmax), ALU.subtract))
                assert step[0] == RV_EXP
                yield
                wait(e, "ra", g + 1)
                rlink(e.reduce_sum(lsum[:, :], le[:, :, :], AX_X))
                rlink(e.reciprocal(lrec[:, :], lsum[:, :]))
                rlink(e.tensor_tensor(score[:, :, :], le[:, :, :], over_experts(lrec), ALU.mult))
                settle(e)
                for t in range(TG):
                    last = e.max(top[:, t, :], score[:, t, :])
                rlink(last)
                yield
                settle(e)
                for t in range(TG):
                    last = e.max_index(topi[:, t, :], top[:, t, :], score[:, t, :])
                rlink(last)
                rlink(e.tensor_copy(topf[:, :, :], topi[:, :, :]))
                rlink(e.reduce_sum(tsum[:, :], top[:, :, 0:2], AX_X))
                rlink(e.tensor_scalar(tsum[:, :], tsum[:, :], 1e-20, None, ALU.add))
                yield
                rlink(e.reciprocal(trec[:, :], tsum[:, :]))
                rlink(e.tensor_tensor(topw[:, :, :], top[:, :, 0:2], trec[:, :].rearrange("p (t o) -> p t o", o=1).to_broadcast([P, TG, 2]), ALU.mult))
                for r in range(2):
                    for t in range(TG):
                        last = (e.tensor_scalar(wk[:, r, t, :], iota_e[:, :], topf[:, t, r:r + 1], topw[:, t, r:r + 1], ALU.is_equal, ALU.mult))
                rlink(last)
                yield
                rlink(e.tensor_tensor(wf[:, :, :], wk[:, 0, :, :], wk[:, 1, :, :], ALU.add))
                rlink(e.tensor_copy(wr[:, :, :], wf[:, :, :]))
                wait(e, "wT_t", g)
                rlink(e.tensor_copy(wst[:, :, 0:E], wr[:, :, :].bitcast(F32)))
                done(e.tensor_tensor(wst[:, :, E:2 * E], wf[:, :, :], wr[:, :, :].bitcast(F32), ALU.subtract), "wst")
                assert step[0] == RV_PER_GROUP
                yield

            tokens(0)
            x_lower(0)
            logits(0)
            for _part in router(0):
                pass

            def group(g, more):
                def unit(u):
                    n = U * g + u
                    par = u % 2
                    wait(e, "gs", n + 1)
                    wait(e, "hw", n)
                    done(e.scalar_tensor_tensor(lk[:, :], gs[:, :], 0.01, gs[:, :], ALU.mult, ALU.max), "lk")
                    wait(e, "lk", n + 1)
                    wait(e, "up_t", n + 1)
                    if u >= 2:
                        wait(e, "hl", n - 1)
                    else:
                        wait(e, "hl", n)
                        wait(e, "fl", FB * g)
                    if u < NS:
                        done(e.tensor_tensor(hw[:, par, :], lk[:, :], bank[6 + par][:, :], ALU.mult), "hw")
                    else:
                        done(e.tensor_tensor(hu[:, :], lk[:, :], bank[6 + par][:, :], ALU.mult), "hu")
                        wait(e, "hu", E * g + u - NS + 1)
                        wait(e, "wb_t", E * g + u - NS + 1)
                        done(e.tensor_tensor(hw[:, par, :], hu[:, :], bank[2][:, :], ALU.mult), "hw")

                for u in range(U):
                    unit(u)
                    if u == NS + 1 and more:
                        tokens(g + 1)
                    if isinstance(g, int) and g == 0 and u in DENSE_AT:
                        split_dense(DENSE_AT.index(u))
                if more:
                    x_lower(g + 1)
                for k in range(KD):
                    wait(e, "yT_h", KD * g + k + 1)
                    subtract(yT_l[:, k, :], bank[k][:, :], yT_h[:, k, :], "yT_l")
                if more:
                    logits(g + 1)
                    parts = router(g + 1)
                for j in range(FB):
                    wait(e, "f1_t", FB * g + j + 1)
                    if j >= 2:
                        wait(e, "fl", FB * g + j - 1)
                    else:
                        wait(e, "hl", U * g + U)
                    done(e.tensor_scalar(hw[:, j % 2, :], bank[4 + j % 2][:, :], b1c[:, j:j + 1], 0.0, ALU.add, ALU.max), "fr")
                    if more and 0 < j < FB - 2:
                        next(parts)
                wait(e, "xb", g + 1)
                wait(e, "st_out", 16 * g)
                for c in range(2):
                    wait(e, "f2_c", 2 * g + c + 1)
                    done(e.tensor_tensor(obuf[:, 2 * c:2 * c + 2, :], bank[6 + c][:, :].rearrange("p (t n) -> p t n", t=2),
                                         xb[:, 2 * c:2 * c + 2, :], ALU.add), "obuf")

            groups(e, group)

        @block.tensor
        def _(e):
            wait(e, "p_const", 1)
            dma_wait(e, "ld_mlp", 8)
            for n in range(2):
                wait(e, "a_sil", n + 1)
                for k in range(KD):
                    last = e.transpose(bank[0][:, k * DH:(k + 1) * DH], h1[:, k * P:(k + 1) * P], ident[0:DH, 0:DH])
                done(last, "t_hT")
                wait(e, "v_hT", n + 1)
                for k in range(KD):
                    last = e.matmul(bank[7][0:DH, 0:(D, H)[n]], hT[:, k, :], (raw_w1, w2p)[n][:, k, :], start=k == 0, stop=k == KD - 1)
                done(last, "t_mlp")
            wait(e, "v_lin", 2)
            done(e.transpose(bank[0][0:H, 0:DH], relp[:, :], ident[0:DH, 0:DH]), "t_rel")
            dma_wait(e, "ld_att", 5)
            for k in range(KD):
                for j in range(KD):
                    last = e.transpose(bank[5][:, k * D + j * P:k * D + (j + 1) * P], raw_att[:, 3, j, k * P:(k + 1) * P], ident[:, :])
            done(last, "t_woT")
            for i in range(KD):
                for k in range(KD):
                    last = e.matmul(bank[1 + i][:, 0:D], raw_att[:, 0, k, i * P:(i + 1) * P], raw_att[:, 1, k, :], start=k == 0, stop=k == KD - 1)
            done(last, "t_mqk")
            wait(e, "v_woT", 1)
            for i in range(KD):
                for k in range(KD):
                    last = e.matmul(bank[3 + i][:, 0:D], raw_att[:, 2, k, i * P:(i + 1) * P], woT[:, k, :], start=k == 0, stop=k == KD - 1)
            done(last, "t_vo")
            dma_wait(e, "ld_null", H + 2)
            dma_wait(e, "ld_out", 1)
            for c in range(HP):
                last = e.matmul(bank[6][0:H, 0:D], nvsel[:, c, :], raw_out[:, c, :], start=c == 0, stop=c == HP - 1)
            done(last, "t_nvw")
            wait(e, "v_wvof", 1)
            wait(e, "v_mqk", KD)
            wait(e, "a_nvw", 1)
            wait(e, "v_rel", 1)

            def body(i, par, live, part):
                if live(-2):
                    wait(e, "oT_l", 2 * (i - 1))
                    wait(e, "pnT", i - 1)
                    for c in range(HP):
                        split_passes(e, bank[6][:, 0:D], (oT_h[:, c, :], oT_l[:, c, :]), (wout_h[:, c, :], wout_l[:, c, :]), c == 0, False)
                    done(e.matmul(bank[6][:, 0:D], pnT[:, :], nvw[:, :], start=False, stop=True), "wo_t")
                if live(0):
                    wait(e, "kn2", i + 1)
                    wait(e, "znT", i - 2)
                    done(e.transpose(bank[0][:, 0:P], kn2[:, :, :].rearrange("p a d -> p (a d)"), ident[:, :]), "kT_t")
                    wait(e, "qn", i + 1)
                    wait(e, "x1", i - 3)
                    wait(e, "uT", i - 2)
                    for c in range(2):
                        for j in range(4):
                            h = 8 * c + 2 * j
                            last = e.transpose(bank[4 + c][:, j * P:(j + 1) * P], qn[:, h:h + 2, :].rearrange("p h d -> p (h d)"), ident[:, :])
                        done(last, "qT_t")
                if live(1):
                    wait(e, "xn", i + 2)
                    wait(e, "kT", i + 1)
                    for k in range(KD):
                        last = e.transpose(bank[0][:, k * P:(k + 1) * P], xn[:, k * P:(k + 1) * P], ident[:, :])
                    done(last, "xnT")
                if live(-3):
                    wait(e, "uT", i - 2)
                    wait(e, "oT_l", 2 * (i - 1) if live(-2) else 2 * NT)
                    for k in range(KD):
                        last = e.matmul(bank[7][:, 0:P], znT[:, k, :], uT[:, k, :], start=k == 0, stop=k == KD - 1)
                    done(last, "sc_t")
                if live(0):
                    wait(e, "kblk", i + 1)
                    wait(e, "qT", 2 * (i + 1))
                    wait(e, "vblk", i + 1)
                    for c in range(HP):
                        for b in range(2):
                            last = e.matmul(bank[1 + c // PB][b * S:(b + 1) * S, (c % PB) * 2 * NK:(c % PB + 1) * 2 * NK],
                                            qT[:, c, b * S:(b + 1) * S], kblk[:, b, :], start=True, stop=True)
                        if c % PB == PB - 1 or c == HP - 1:
                            done(last, "sim_t")
                if live(-3):
                    wait(e, "at", i - 2)
                    for k in range(KD):
                        last = e.matmul(bank[7][:, k * P:(k + 1) * P], zn[:, 1 - par, k * P:(k + 1) * P], at[:, :], start=True, stop=True)
                    done(last, "rt_t")
                if live(-1):
                    wait(e, "pr", i)
                    wait(e, "qT", 2 * (i + 1) if live(0) else 2 * NT)
                    wait(e, "xnT_l", i + 2 if live(1) else NT)
                    for c in range(2):
                        for j in range(4):
                            h = 8 * c + 2 * j
                            last = e.transpose(bank[4 + c][:, j * P:(j + 1) * P], pr[:, h * S:(h + 2) * S], ident[:, :])
                        done(last, "pT_t")
                    done(e.transpose(bank[0][0:H, 0:P], pr[:, H * S:H * NK], ident[:, :]), "pnT_t")
                if live(1):
                    wait(e, "xnT_l", i + 2)
                    for c in range(NB3):
                        wait(e, "sim", NB3 * i + c + 1)
                        for k in range(KD):
                            last = split_passes(e, bank[1 + c][:, 0:QB], (xnT_h[:, k, :], xnT_l[:, k, :]),
                                                (wqkv_h[:, k, c * QB:(c + 1) * QB], wqkv_l[:, k, c * QB:(c + 1) * QB]), k == 0, k == KD - 1)
                        done(last, "qkv")
                if live(-1):
                    wait(e, "pT_l", 2 * i)
                    wait(e, "vblk", i)
                    wait(e, "zn", i - 1)
                    wait(e, "rT_l", i - 2)
                    for b in range(2):
                        last = split_passes(e, bank[6 + b][:, :], (vblk_h[:, 1 - par, b, :], vblk_l[:, 1 - par, b, :]),
                                            (pT_h[:, :, b * S:(b + 1) * S], pT_l[:, :, b * S:(b + 1) * S]), True, True)
                        done(last, "av_t")
                if live(-2):
                    wait(e, "zn", i - 1)
                    wait(e, "pnT", i if live(-1) else NT)
                    wait(e, "xnT_l", i + 2 if live(1) else NT)
                    for k in range(KD):
                        last = e.transpose(bank[0][:, k * P:(k + 1) * P], zn[:, par, k * P:(k + 1) * P], ident[:, :])
                    done(last, "znT_t")
                if live(-3):
                    wait(e, "rT_l", i - 2)
                    wait(e, "pT_l", 2 * i if live(-1) else 2 * NT)
                    for k in range(KD):
                        last = split_passes(e, bank[4][:, 0:D], (rT_h[:, k, :], rT_l[:, k, :]), (wvo_h[:, k, :], wvo_l[:, k, :]), k == 0, k == KD - 1)
                    done(last, "vo_t")
                if live(-2):
                    wait(e, "znT", i - 1)
                    wait(e, "pT_l", 2 * i if live(-1) else 2 * NT)
                    for j in range(KD):
                        for k in range(KD):
                            last = e.matmul(bank[5][:, j * P:(j + 1) * P], mqk[:, k, j * P:(j + 1) * P], znT[:, k, :], start=k == 0, stop=k == KD - 1)
                    done(last, "uT_t")

            wait(e, "v_wvo", 1)
            wait(e, "v_wout", 1)
            wait(e, "p_dec", 1)
            wait(e, "p_nkk", 1)
            pipeline(e, body)

            wait(e, "unit", U)
            wait(e, "p_sel", 1)
            wait(e, "v_wtl", 1)
            wait(e, "x1", NT)

            def x_parts(k):
                return x1T_h[:, k, :], x1T_l[:, k, :]

            def x_transpose(g):
                wait(e, "xg", g + 1)
                wait(e, "gs", U * g)
                for k in range(KD):
                    for t in range(TG):
                        last = e.transpose(bank[4 + k][:, t * P:(t + 1) * P], xg[:, t, k * P:(k + 1) * P], ident[:, :])
                    done(last, "x1T_t")

            def logits(g, k):
                wait(e, "x1T_l", KD * (g + 1))
                split_passes(e, bank[3][:, :], (wt_h[:, k, :], wt_l[:, k, :]), x_parts(k), k == 0, False)
                if k == KD - 1:
                    done(e.matmul(bank[3][:, :], wgT[:, :], condT[:, span(g * SB, SB)].rearrange("c (s o) -> c s o", o=1).to_broadcast([DH, SB, S]),
                                  start=False, stop=True), "lg_t")

            def logits_transpose(g):
                wait(e, "lgT", g + 1)
                wait(e, "hw", U * g)
                for t in range(TG):
                    last = e.matmul(bank[2][:, t * E:(t + 1) * E], lgT[:, t * P:(t + 1) * P], ident[0:E, 0:E], start=True, stop=True)
                done(last, "lgtr")

            def weights_transpose(g):
                wait(e, "wst", g + 1)
                for t in range(TG):
                    last = e.transpose(bank[3][0:2 * E, t * P:(t + 1) * P], wst[:, t, :], ident[:, :])
                done(last, "wT_t")

            x_transpose(0)
            for k in range(KD):
                logits(0, k)
            logits_transpose(0)

            def group(g, more):
                def gate_up(u):
                    n = U * g + u
                    par = u % 2
                    if u < 2:
                        wait(e, "fr", FB * g)
                    else:
                        wait(e, "gs", n - 1)
                    for o, name, b in ((0, "gate_t", 4), (D, "up_t", 6)):
                        if b == 6:
                            if u < 2:
                                wait(e, "obuf", 2 * (g - 1) + par + 1)
                            elif u - 2 < NS:
                                wait(e, "hw", n - 1)
                            else:
                                wait(e, "hu", E * g + u - 2 - NS + 1)
                        for k in range(KD):
                            w = slice(o + k * M, o + (k + 1) * M)
                            last = split_passes(e, bank[b + par][:, :], (wu_h[:, u, w], wu_l[:, u, w]), x_parts(k), k == 0, k == KD - 1)
                        done(last, name)

                def down(u):
                    wait(e, "hl", U * g + u + 1)
                    if u == 0:
                        wait(e, "yT_l", KD * g)
                    for k in range(KD):
                        w = slice(2 * D + k * P, 2 * D + (k + 1) * P)
                        last = split_passes(e, bank[k][:, :], (wu_h[:, u, w], wu_l[:, u, w]), (hh[:, u % 2, :], hl[:, u % 2, :]), u == 0, u == U - 1)
                    done(last, "down_t")

                def spread(u):
                    wait(e, "wT", g + 1)
                    wait(e, "hw", U * g + u)
                    done(e.matmul(bank[2][:, :], sel[:, u - NS, :], wT[:, :], start=True, stop=True), "wb_t")

                for u in range(U):
                    gate_up(u)
                    if isinstance(g, int) and g == 0 and u == 1:
                        weights_transpose(0)
                    if u >= NS:
                        spread(u)
                    if u >= 2:
                        down(u - 2)
                if more:
                    x_transpose(g + 1)
                down(U - 2)
                if more:
                    logits(g + 1, 0)
                down(U - 1)
                if more:
                    logits(g + 1, 1)

                y_parts = [(yT_h[:, k, :], yT_l[:, k, :]) for k in range(KD)]
                wait(e, "yT_l", KD * (g + 1))
                wait(e, "f_l", 4)

                def first(j):
                    if j >= 2:
                        wait(e, "fr", FB * g + j - 1)
                    for k in range(KD):
                        last = split_passes(e, bank[4 + j % 2][:, :], (w1_h[:, k, j * P:(j + 1) * P], w1_l[:, k, j * P:(j + 1) * P]),
                                            y_parts[k], k == 0, k == KD - 1)
                    done(last, "f1_t")

                def second(j):
                    wait(e, "fl", FB * g + j + 1)
                    for t in range(TG):
                        last = split_passes(e, bank[6 + t // 2][:, (t % 2) * D:(t % 2 + 1) * D],
                                            (hh[:, j % 2, t * P:(t + 1) * P], hl[:, j % 2, t * P:(t + 1) * P]),
                                            (w2_h[:, j, :], w2_l[:, j, :]), j == 0 and t % 2 == 0, j == FB - 1, skip_group_check=True)
                        if j == FB - 1 and t % 2 == 1:
                            done(last, "f2_c")
                    if j < FB - 1:
                        done(last, "f2_t")

                for j in range(FB + 2):
                    if j < FB:
                        first(j)
                    if j == 1 and more:
                        logits_transpose(g + 1)
                    if j == FB + 1 and more:
                        weights_transpose(g + 1)
                    if j >= 2:
                        second(j - 2)

            groups(e, group)


_SHORT = {
    "x": "x", "cond": "cond_64", "mask": "mask_BxS_bf1",
    "c_g_norm": "L0_cond_g_norm", "c_Wq": "L0_cond_Wq", "c_Wkv": "L0_cond_Wkv", "c_q_scale": "L0_cond_q_scale",
    "c_k_scale": "L0_cond_k_scale", "c_nullb": "L0_cond_null_attn_bias", "c_w0": "L0_cond_w0", "c_b0": "L0_cond_b0",
    "c_g0": "L0_cond_g0", "c_w1": "L0_cond_w1", "c_b1": "L0_cond_b1", "c_g1": "L0_cond_g1", "c_w2": "L0_cond_w2",
    "c_b2": "L0_cond_b2", "c_Wout": "L0_cond_Wout", "c_g_out": "L0_cond_g_out",
    "t_Wq": "L0_attn_Wq", "t_Wk": "L0_attn_Wk", "t_Wv": "L0_attn_Wv", "t_Wo": "L0_attn_Wo",
    "t_decay": "L0_attn_decay_logit", "t_oscale": "L0_attn_out_scale",
    "m_wt": "L0_cond2_wt", "m_wg": "L0_cond2_wg", "m_wgate": "L0_cond2_w_gate", "m_wup": "L0_cond2_w_up",
    "m_wdown": "L0_cond2_w_down", "m_sg": "L0_cond2_sw_gate", "m_su": "L0_cond2_sw_up", "m_sd": "L0_cond2_sw_down",
    "f_W1": "L0_ffn_W1", "f_b1": "L0_ffn_b1", "f_W2": "L0_ffn_W2", "f_b2": "L0_ffn_b2",
}


def kernel(**inputs):
    import numpy as np
    import concourse.bacc as bacc
    from concourse.bass_utils import run_bass_kernel_spmd

    nc = bacc.Bacc("TRN2", target_bir_lowering=False, num_devices=1)
    arrays, aps = {}, {}
    for short, name in _SHORT.items():
        v = np.ascontiguousarray(inputs[name])
        if v.ndim == 0 or short in ("t_decay", "t_oscale"):
            v = v.reshape(1, 1)
        if v.dtype == np.bool_:
            v = v.view(np.uint8)
        arrays["in_" + short] = v
        aps[short] = nc.dram_tensor("in_" + short, v.shape, mybir.dt.from_np(v.dtype), kind="ExternalInput").ap()
    out = nc.dram_tensor("out", (B, S, D), F32, kind="ExternalOutput").ap()
    adaln_attention_ffn(nc, aps, out)
    r = run_bass_kernel_spmd(nc, [arrays], core_ids=[0])
    return r.results[0]["out"]
```
